# Optimizing a Trainium2 kernel written in Bass

```python
import numpy as np
import jax
import jax.numpy as jnp

def _softmax(x, axis=-1):
    return jax.nn.softmax(x, axis=axis)

def _gelu(x):
    return jax.nn.gelu(x, approximate=True)

def _silu(x):
    return jax.nn.silu(x)

def _sigmoid(x):
    return jax.nn.sigmoid(x)

def _layernorm(x, axis=-1, eps=1e-05):
    m = jnp.mean(x, axis=axis, keepdims=True)
    v = jnp.var(x, axis=axis, keepdims=True)
    return (x - m) / jnp.sqrt(v + eps)

def _scatter_add(tgt, idx, src, axis=0):
    return tgt.at[idx].add(src)

def _segment_sum(src, seg, n):
    return jax.ops.segment_sum(src, seg, n)
kernel_name = 'mk_hybrid_d2_jaxref_r8_a3bcbf'

def setup_inputs(seed: int=0):
    np.random.seed(seed)
    _w = jnp.asarray

    def _L0_attn_a_setup():
        import jax, jax.numpy as jnp
        import numpy as np
        H = 4
        M = 64
        EPS = 1e-05
        CLAMP = 32.0

        def _rope(x):
            B, T, Hh, D = x.shape
            half = D // 2
            inv_freq = 1.0 / 10000.0 ** (jnp.arange(half, dtype=jnp.float32) / half)
            ang = jnp.arange(T, dtype=jnp.float32)[:, None] * inv_freq[None, :]
            cos = jnp.cos(ang)[None, :, None, :]
            sin = jnp.sin(ang)[None, :, None, :]
            x1, x2 = (x[..., :half], x[..., half:])
            return jnp.concatenate([x1 * cos - x2 * sin, x2 * cos + x1 * sin], axis=-1)

        def _forward(hidden_states, Wq, Wk, Wv, Wg, Wo, sk_w1, sk_w2, sk_b2, sv_w1, sv_w2, sv_b2, gnorm_w):
            x = hidden_states
            B, T, D = x.shape
            Dk = D // H
            Dv = D // H
            q = (x @ Wq).reshape(B, T, H, Dk)
            k = (x @ Wk).reshape(B, T, H, Dk)
            v = (x @ Wv).reshape(B, T, H, Dv)
            q = _rope(q)
            k = _rope(k)
            q = q.transpose(0, 2, 1, 3)
            k = k.transpose(0, 2, 1, 3)
            v = v.transpose(0, 2, 1, 3)
            sk = jnp.clip(x @ sk_w1 @ sk_w2 + sk_b2, -CLAMP, CLAMP).reshape(B, T, H, M).transpose(0, 2, 1, 3)
            sv = jnp.clip(x @ sv_w1 @ sv_w2 + sv_b2, -CLAMP, CLAMP).reshape(B, T, H, M).transpose(0, 2, 1, 3)
            scale = Dk ** (-0.5)
            mask = jnp.tril(jnp.ones((T, T), dtype=bool))
            wk = jnp.exp(sk)
            zk = jnp.cumsum(wk, axis=2)
            S = jnp.einsum('bhtd,bhsd->bhts', q, k)
            S = jnp.where(mask, S, 0.0)
            logits = jnp.einsum('bhts,bhsm->bhtm', S, wk) * scale / zk
            p = jax.nn.softmax(logits, axis=-1)
            wv = jnp.exp(sv)
            zv = jnp.cumsum(wv, axis=2)
            A = jnp.einsum('bhtm,bhsm->bhts', p / zv, wv)
            A = jnp.where(mask, A, 0.0)
            o = jnp.einsum('bhts,bhsd->bhtd', A, v)
            o = o.transpose(0, 2, 1, 3)
            g = (x @ Wg).reshape(B, T, H, Dv)
            on = o * jax.lax.rsqrt(jnp.mean(o * o, axis=-1, keepdims=True) + EPS) * gnorm_w
            o = on * g * jax.nn.sigmoid(g)
            return o.reshape(B, T, H * Dv) @ Wo
        key = jax.random.key(seed)
        ks = jax.random.split(key, 10)
        B, T, D = (2, 256, 128)
        low = 16

        def w(k, shape, s=0.02):
            return jax.random.normal(k, shape, dtype=jnp.float32) * s
        return {'hidden_states': jax.random.normal(ks[0], (B, T, D), dtype=jnp.float32), 'Wq': w(ks[1], (D, D)), 'Wk': w(ks[2], (D, D)), 'Wv': w(ks[3], (D, D)), 'Wg': w(ks[4], (D, D)), 'Wo': w(ks[5], (D, D)), 'sk_w1': w(ks[6], (D, low)), 'sk_w2': w(ks[7], (low, H * M)), 'sk_b2': jnp.zeros((H * M,), dtype=jnp.float32), 'sv_w1': w(ks[8], (D, low)), 'sv_w2': w(ks[9], (low, H * M)), 'sv_b2': jnp.zeros((H * M,), dtype=jnp.float32), 'gnorm_w': jnp.ones((D // H,), dtype=jnp.float32)}
    _L0_attn_a_in = _L0_attn_a_setup()

    def _L0_attn_b_setup():
        import math
        import jax, jax.numpy as jnp
        import numpy as np
        B, S, DIM, HEADS = (1, 256, 128, 16)
        HEAD_DIM = DIM // HEADS
        key = jax.random.key(seed)
        ks = jax.random.split(key, 6)
        scale = DIM ** (-0.5)
        x = jax.random.normal(ks[0], (B, S, DIM), jnp.float32)
        wq = jax.random.normal(ks[1], (DIM, DIM), jnp.float32) * scale
        wk = jax.random.normal(ks[2], (DIM, DIM), jnp.float32) * scale
        wv = jax.random.normal(ks[3], (DIM, DIM), jnp.float32) * scale
        wo = jax.random.normal(ks[4], (DIM, DIM), jnp.float32) * scale
        pope_bias = -jax.random.uniform(ks[5], (HEADS, HEAD_DIM), jnp.float32) * 3.0
        return {'x': x, 'wq': wq, 'wk': wk, 'wv': wv, 'wo': wo, 'pope_bias': pope_bias}
    _L0_attn_b_in = _L0_attn_b_setup()

    def _L0_ffn_setup():
        import jax, jax.numpy as jnp
        import numpy as np
        B, S, D, O, E, R, TOP_K = (4, 128, 128, 128, 8, 16, 2)
        SCALING = 32.0 / 16.0
        NEG_INF = -1000000000.0
        key = jax.random.key(seed)
        ks = jax.random.split(key, 6)
        return {'x': jax.random.normal(ks[0], (B, S, D), jnp.float32), 'base_w': jax.random.normal(ks[1], (O, D), jnp.float32) * 0.02, 'base_b': jnp.zeros((O,), jnp.float32), 'lora_A': jax.random.normal(ks[2], (E, D, R), jnp.float32) * 0.02, 'lora_B': jax.random.normal(ks[3], (E, R, O), jnp.float32) * 0.02, 'router_w': jax.random.normal(ks[4], (E, D), jnp.float32) * 0.02, 'router_b': jnp.zeros((E,), jnp.float32)}
    _L0_ffn_in = _L0_ffn_setup()

    def _L1_attn_a_setup():
        import jax, jax.numpy as jnp
        import numpy as np
        NUM_HEADS = 16
        key = jax.random.key(seed)
        k1, k2, k3, k4 = jax.random.split(key, 4)
        d_model = 128
        B, S = (4, 256)
        scale = 1.0 / np.sqrt(d_model)
        x = jax.random.normal(k1, (B, S, d_model), dtype=jnp.float32)
        W_k = jax.random.normal(k2, (d_model, d_model), dtype=jnp.float32) * scale
        W_v = jax.random.normal(k3, (d_model, d_model), dtype=jnp.float32) * scale
        W_o = jax.random.normal(k4, (d_model, d_model), dtype=jnp.float32) * scale
        return {'x': x, 'W_k': W_k, 'W_v': W_v, 'W_o': W_o}
    _L1_attn_a_in = _L1_attn_a_setup()

    def _L1_attn_b_setup():
        import jax, jax.numpy as jnp
        import numpy as np
        B, S, DM, H = (4, 128, 128, 16)
        D = DM // H

        def _split_heads(x):
            return x.reshape(x.shape[0], x.shape[1], H, D).transpose(0, 2, 1, 3)
        key = jax.random.key(seed)
        ks = jax.random.split(key, 16)
        sc = 0.02
        return {'hidden_states': jax.random.normal(ks[0], (B, S, DM), jnp.float32), 'wq': jax.random.normal(ks[1], (DM, DM), jnp.float32) * sc, 'bq': jax.random.normal(ks[2], (DM,), jnp.float32) * sc, 'wk': jax.random.normal(ks[3], (DM, DM), jnp.float32) * sc, 'bk': jax.random.normal(ks[4], (DM,), jnp.float32) * sc, 'wv': jax.random.normal(ks[5], (DM, DM), jnp.float32) * sc, 'bv': jax.random.normal(ks[6], (DM,), jnp.float32) * sc, 'wo': jax.random.normal(ks[7], (DM, DM), jnp.float32) * sc, 'bo': jax.random.normal(ks[8], (DM,), jnp.float32) * sc, 'wfq': jax.random.normal(ks[9], (DM, DM), jnp.float32) * sc, 'bfq': jax.random.normal(ks[10], (DM,), jnp.float32) * sc, 'wfg': jax.random.normal(ks[11], (DM, DM), jnp.float32) * sc, 'bfg': jax.random.normal(ks[12], (DM,), jnp.float32) * sc, 'up': jax.random.normal(ks[13], (H, 1, D), jnp.float32) * sc, 'uz': jax.random.normal(ks[14], (H, 1, D), jnp.float32) * sc}
    _L1_attn_b_in = _L1_attn_b_setup()

    def _L1_ffn_setup():
        import jax, jax.numpy as jnp
        import numpy as np

        def _bitlinear(x, w_latent):
            scale = jax.lax.stop_gradient(jnp.clip(jnp.mean(jnp.abs(w_latent), axis=1, keepdims=True), 1e-05, None))
            tern = jnp.clip(jnp.round(w_latent / scale), -1.0, 1.0)
            w = w_latent + jax.lax.stop_gradient(tern - w_latent)
            return x @ (w * scale).T
        key = jax.random.key(seed)
        ks = jax.random.split(key, 6)
        dim, hidden, rank = (128, 512, 16)
        B, S = (4, 512)
        x = jax.random.normal(ks[0], (B, S, dim), dtype=jnp.float32)
        w_fc = 0.02 * jax.random.normal(ks[1], (hidden, dim), dtype=jnp.float32)
        w_proj = 0.02 * jax.random.normal(ks[2], (dim, hidden), dtype=jnp.float32)
        u = 0.02 * jax.random.normal(ks[3], (hidden, rank), dtype=jnp.float32)
        v = 0.02 * jax.random.normal(ks[4], (rank, dim), dtype=jnp.float32)
        fast_b = jax.random.normal(ks[5], (rank, rank), dtype=jnp.float32)
        gate = jnp.float32(0.05)
        return {'x': x, 'fast_b': fast_b, 'w_fc': w_fc, 'w_proj': w_proj, 'u': u, 'v': v, 'gate': gate}
    _L1_ffn_in = _L1_ffn_setup()
    _d = {'L0_attn_a_hidden_states': _L0_attn_a_in['hidden_states'], 'L0_attn_a_Wq': _L0_attn_a_in['Wq'], 'L0_attn_a_Wk': _L0_attn_a_in['Wk'], 'L0_attn_a_Wv': _L0_attn_a_in['Wv'], 'L0_attn_a_Wg': _L0_attn_a_in['Wg'], 'L0_attn_a_Wo': _L0_attn_a_in['Wo'], 'L0_attn_a_sk_w1': _L0_attn_a_in['sk_w1'], 'L0_attn_a_sk_w2': _L0_attn_a_in['sk_w2'], 'L0_attn_a_sk_b2': _L0_attn_a_in['sk_b2'], 'L0_attn_a_sv_w1': _L0_attn_a_in['sv_w1'], 'L0_attn_a_sv_w2': _L0_attn_a_in['sv_w2'], 'L0_attn_a_sv_b2': _L0_attn_a_in['sv_b2'], 'L0_attn_a_gnorm_w': _L0_attn_a_in['gnorm_w'], 'L0_attn_b_wq': _L0_attn_b_in['wq'], 'L0_attn_b_wk': _L0_attn_b_in['wk'], 'L0_attn_b_wv': _L0_attn_b_in['wv'], 'L0_attn_b_wo': _L0_attn_b_in['wo'], 'L0_attn_b_pope_bias': _L0_attn_b_in['pope_bias'], 'L0_ffn_base_w': _L0_ffn_in['base_w'], 'L0_ffn_base_b': _L0_ffn_in['base_b'], 'L0_ffn_lora_A': _L0_ffn_in['lora_A'], 'L0_ffn_lora_B': _L0_ffn_in['lora_B'], 'L0_ffn_router_w': _L0_ffn_in['router_w'], 'L0_ffn_router_b': _L0_ffn_in['router_b'], 'L1_attn_a_W_k': _L1_attn_a_in['W_k'], 'L1_attn_a_W_v': _L1_attn_a_in['W_v'], 'L1_attn_a_W_o': _L1_attn_a_in['W_o'], 'L1_attn_b_wq': _L1_attn_b_in['wq'], 'L1_attn_b_bq': _L1_attn_b_in['bq'], 'L1_attn_b_wk': _L1_attn_b_in['wk'], 'L1_attn_b_bk': _L1_attn_b_in['bk'], 'L1_attn_b_wv': _L1_attn_b_in['wv'], 'L1_attn_b_bv': _L1_attn_b_in['bv'], 'L1_attn_b_wo': _L1_attn_b_in['wo'], 'L1_attn_b_bo': _L1_attn_b_in['bo'], 'L1_attn_b_wfq': _L1_attn_b_in['wfq'], 'L1_attn_b_bfq': _L1_attn_b_in['bfq'], 'L1_attn_b_wfg': _L1_attn_b_in['wfg'], 'L1_attn_b_bfg': _L1_attn_b_in['bfg'], 'L1_attn_b_up': _L1_attn_b_in['up'], 'L1_attn_b_uz': _L1_attn_b_in['uz'], 'L1_ffn_fast_b': _L1_ffn_in['fast_b'], 'L1_ffn_w_fc': _L1_ffn_in['w_fc'], 'L1_ffn_w_proj': _L1_ffn_in['w_proj'], 'L1_ffn_u': _L1_ffn_in['u'], 'L1_ffn_v': _L1_ffn_in['v'], 'L1_ffn_gate': _L1_ffn_in['gate']}
    _x0 = _d['L0_attn_a_hidden_states']
    _d['L0_attn_a_hidden_states'] = jax.random.normal(jax.random.fold_in(jax.random.key(seed), 1), (8, 512, 128), dtype=_x0.dtype)
    del _x0
    return _d

def reference(L0_attn_a_hidden_states, L0_attn_a_Wq, L0_attn_a_Wk, L0_attn_a_Wv, L0_attn_a_Wg, L0_attn_a_Wo, L0_attn_a_sk_w1, L0_attn_a_sk_w2, L0_attn_a_sk_b2, L0_attn_a_sv_w1, L0_attn_a_sv_w2, L0_attn_a_sv_b2, L0_attn_a_gnorm_w, L0_attn_b_wq, L0_attn_b_wk, L0_attn_b_wv, L0_attn_b_wo, L0_attn_b_pope_bias, L0_ffn_base_w, L0_ffn_base_b, L0_ffn_lora_A, L0_ffn_lora_B, L0_ffn_router_w, L0_ffn_router_b, L1_attn_a_W_k, L1_attn_a_W_v, L1_attn_a_W_o, L1_attn_b_wq, L1_attn_b_bq, L1_attn_b_wk, L1_attn_b_bk, L1_attn_b_wv, L1_attn_b_bv, L1_attn_b_wo, L1_attn_b_bo, L1_attn_b_wfq, L1_attn_b_bfq, L1_attn_b_wfg, L1_attn_b_bfg, L1_attn_b_up, L1_attn_b_uz, L1_ffn_fast_b, L1_ffn_w_fc, L1_ffn_w_proj, L1_ffn_u, L1_ffn_v, L1_ffn_gate):

    def _L0_attn_a_ref(hidden_states, Wq, Wk, Wv, Wg, Wo, sk_w1, sk_w2, sk_b2, sv_w1, sv_w2, sv_b2, gnorm_w):
        import jax, jax.numpy as jnp
        import numpy as np
        H = 4
        M = 64
        EPS = 1e-05
        CLAMP = 32.0

        def _rope(x):
            B, T, Hh, D = x.shape
            half = D // 2
            inv_freq = 1.0 / 10000.0 ** (jnp.arange(half, dtype=jnp.float32) / half)
            ang = jnp.arange(T, dtype=jnp.float32)[:, None] * inv_freq[None, :]
            cos = jnp.cos(ang)[None, :, None, :]
            sin = jnp.sin(ang)[None, :, None, :]
            x1, x2 = (x[..., :half], x[..., half:])
            return jnp.concatenate([x1 * cos - x2 * sin, x2 * cos + x1 * sin], axis=-1)

        def _forward(hidden_states, Wq, Wk, Wv, Wg, Wo, sk_w1, sk_w2, sk_b2, sv_w1, sv_w2, sv_b2, gnorm_w):
            x = hidden_states
            B, T, D = x.shape
            Dk = D // H
            Dv = D // H
            q = (x @ Wq).reshape(B, T, H, Dk)
            k = (x @ Wk).reshape(B, T, H, Dk)
            v = (x @ Wv).reshape(B, T, H, Dv)
            q = _rope(q)
            k = _rope(k)
            q = q.transpose(0, 2, 1, 3)
            k = k.transpose(0, 2, 1, 3)
            v = v.transpose(0, 2, 1, 3)
            sk = jnp.clip(x @ sk_w1 @ sk_w2 + sk_b2, -CLAMP, CLAMP).reshape(B, T, H, M).transpose(0, 2, 1, 3)
            sv = jnp.clip(x @ sv_w1 @ sv_w2 + sv_b2, -CLAMP, CLAMP).reshape(B, T, H, M).transpose(0, 2, 1, 3)
            scale = Dk ** (-0.5)
            mask = jnp.tril(jnp.ones((T, T), dtype=bool))
            wk = jnp.exp(sk)
            zk = jnp.cumsum(wk, axis=2)
            S = jnp.einsum('bhtd,bhsd->bhts', q, k)
            S = jnp.where(mask, S, 0.0)
            logits = jnp.einsum('bhts,bhsm->bhtm', S, wk) * scale / zk
            p = jax.nn.softmax(logits, axis=-1)
            wv = jnp.exp(sv)
            zv = jnp.cumsum(wv, axis=2)
            A = jnp.einsum('bhtm,bhsm->bhts', p / zv, wv)
            A = jnp.where(mask, A, 0.0)
            o = jnp.einsum('bhts,bhsd->bhtd', A, v)
            o = o.transpose(0, 2, 1, 3)
            g = (x @ Wg).reshape(B, T, H, Dv)
            on = o * jax.lax.rsqrt(jnp.mean(o * o, axis=-1, keepdims=True) + EPS) * gnorm_w
            o = on * g * jax.nn.sigmoid(g)
            return o.reshape(B, T, H * Dv) @ Wo
        return _forward(hidden_states, Wq, Wk, Wv, Wg, Wo, sk_w1, sk_w2, sk_b2, sv_w1, sv_w2, sv_b2, gnorm_w)

    def _L0_attn_b_ref(x, wq, wk, wv, wo, pope_bias):
        import math
        import jax, jax.numpy as jnp
        import numpy as np
        B, S, DIM, HEADS = (1, 256, 128, 16)
        HEAD_DIM = DIM // HEADS
        B_, S_, C = x.shape
        H = HEADS
        D = C // H
        q = jnp.einsum('bsc,oc->bso', x, wq).reshape(B_, S_, H, D).transpose(0, 2, 1, 3)
        k = jnp.einsum('bsc,oc->bso', x, wk).reshape(B_, S_, H, D).transpose(0, 2, 1, 3)
        v = jnp.einsum('bsc,oc->bso', x, wv).reshape(B_, S_, H, D).transpose(0, 2, 1, 3)
        inv_freqs = 10000.0 ** (-(jnp.arange(D, dtype=jnp.float32) / D))
        pos = jnp.arange(S_, dtype=jnp.float32)
        freqs = pos[:, None] * inv_freqs[None, :]
        bias = jnp.clip(pope_bias, -2.0 * math.pi, 0.0)
        freqs_with_bias = freqs[None, :, :] + bias[:, None, :]
        q_mag = jax.nn.softplus(q)
        k_mag = jax.nn.softplus(k)
        qp = freqs[None, None, :, :]
        kp = freqs_with_bias[None, :, :, :]
        q_embed = jnp.stack([q_mag * jnp.cos(qp), q_mag * jnp.sin(qp)], axis=-1).reshape(B_, H, S_, 2 * D)
        k_embed = jnp.stack([k_mag * jnp.cos(kp), k_mag * jnp.sin(kp)], axis=-1).reshape(B_, H, S_, 2 * D)
        scores = jnp.einsum('bhsd,bhtd->bhst', q_embed, k_embed) / D ** 0.5
        attn = jax.nn.softmax(scores, axis=-1)
        out = jnp.einsum('bhst,bhtd->bhsd', attn, v)
        out = out.transpose(0, 2, 1, 3).reshape(B_, S_, C)
        return jnp.einsum('bsc,oc->bso', out, wo)

    def _L0_ffn_ref(x, base_w, base_b, lora_A, lora_B, router_w, router_b):
        import jax, jax.numpy as jnp
        import numpy as np
        B, S, D, O, E, R, TOP_K = (4, 128, 128, 128, 8, 16, 2)
        SCALING = 32.0 / 16.0
        NEG_INF = -1000000000.0
        result = jnp.einsum('bsd,od->bso', x, base_w) + base_b
        ax = jnp.einsum('bsd,edr->bser', x, lora_A)
        bax = jnp.einsum('bser,ero->bseo', ax, lora_B)
        logits = jnp.einsum('bsd,ed->bse', x, router_w) + router_b
        kth = jax.lax.top_k(logits, TOP_K)[0][..., -1:]
        masked = jnp.where(logits < kth, NEG_INF, logits)
        expert_weights = jax.nn.softmax(masked, axis=-1)
        return result + SCALING * jnp.einsum('bse,bseo->bso', expert_weights, bax)

    def _L1_attn_a_ref(x, W_k, W_v, W_o):
        import jax, jax.numpy as jnp
        import numpy as np
        NUM_HEADS = 16
        B, S, D = x.shape
        H = NUM_HEADS
        dk = D // H
        inv_sqrt_dk = 1.0 / jnp.sqrt(jnp.asarray(dk, dtype=x.dtype))
        Q = (x @ W_k.T).reshape(B, S, H, dk).transpose(0, 2, 1, 3)
        sq_norm = jnp.sum(Q * Q, axis=-1, keepdims=True)
        dot = jnp.einsum('bhsk,bhtk->bhst', Q, Q)
        squared_dist = sq_norm - 2.0 * dot + sq_norm.transpose(0, 1, 3, 2)
        scores = -squared_dist * inv_sqrt_dk
        attn = jax.nn.softmax(scores, axis=-1)
        context_q = jnp.einsum('bhst,bhtk->bhsk', attn, Q)
        Wq_h = W_k.reshape(H, dk, D)
        Wv_h = W_v.reshape(H, dk, D)
        merged = jnp.einsum('hkd,hvd->hkv', Wq_h, Wv_h)
        attn_out = jnp.einsum('bhsk,hkv->bhsv', context_q, merged) * inv_sqrt_dk
        attn_out = attn_out.transpose(0, 2, 1, 3).reshape(B, S, D)
        return attn_out @ W_o.T

    def _L1_attn_b_ref(hidden_states, wq, bq, wk, bk, wv, bv, wo, bo, wfq, bfq, wfg, bfg, up, uz):
        import jax, jax.numpy as jnp
        import numpy as np
        B, S, DM, H = (4, 128, 128, 16)
        D = DM // H

        def _split_heads(x):
            return x.reshape(x.shape[0], x.shape[1], H, D).transpose(0, 2, 1, 3)
        key_len = hidden_states.shape[1]
        mixed_q = hidden_states @ wq + bq
        mixed_k = hidden_states @ wk + bk
        mixed_v = hidden_states @ wv + bv
        glo = jnp.mean(mixed_q, axis=1, keepdims=True)
        c = jnp.tanh(mixed_q @ wfq + bfq + (glo @ wfg + bfg))
        c = _split_heads(c)
        p = jnp.sum(c * up[None], axis=-1)
        z = jnp.sum(c * uz[None], axis=-1)
        P = jax.nn.sigmoid(p) * key_len
        Z = jax.nn.sigmoid(z) * key_len
        j = jnp.arange(key_len, dtype=P.dtype)
        G = -(j[None, None, None, :] - P[..., None]) ** 2 * 2.0 / Z[..., None] ** 2
        q = _split_heads(mixed_q)
        k = _split_heads(mixed_k)
        v = _split_heads(mixed_v)
        scores = jnp.einsum('bhqd,bhkd->bhqk', q, k) / jnp.sqrt(jnp.float32(D))
        scores = scores + G
        probs = jax.nn.softmax(scores, axis=-1)
        ctx = jnp.einsum('bhqk,bhkd->bhqd', probs, v)
        ctx = ctx.transpose(0, 2, 1, 3).reshape(ctx.shape[0], key_len, H * D)
        return ctx @ wo + bo

    def _L1_ffn_ref(x, fast_b, w_fc, w_proj, u, v, gate):
        import jax, jax.numpy as jnp
        import numpy as np

        def _bitlinear(x, w_latent):
            scale = jax.lax.stop_gradient(jnp.clip(jnp.mean(jnp.abs(w_latent), axis=1, keepdims=True), 1e-05, None))
            tern = jnp.clip(jnp.round(w_latent / scale), -1.0, 1.0)
            w = w_latent + jax.lax.stop_gradient(tern - w_latent)
            return x @ (w * scale).T
        h = _bitlinear(x, w_fc) + gate * (x @ v.T @ fast_b.T @ u.T)
        r = jnp.maximum(h, 0.0)
        return _bitlinear(r * r, w_proj)
    x = L0_attn_a_hidden_states
    x = x + _L0_attn_a_ref(_layernorm(x, axis=-1), L0_attn_a_Wq, L0_attn_a_Wk, L0_attn_a_Wv, L0_attn_a_Wg, L0_attn_a_Wo, L0_attn_a_sk_w1, L0_attn_a_sk_w2, L0_attn_a_sk_b2, L0_attn_a_sv_w1, L0_attn_a_sv_w2, L0_attn_a_sv_b2, L0_attn_a_gnorm_w)
    x = x + _L0_ffn_ref(_layernorm(x, axis=-1), L0_ffn_base_w, L0_ffn_base_b, L0_ffn_lora_A, L0_ffn_lora_B, L0_ffn_router_w, L0_ffn_router_b)
    x = x + _L0_attn_b_ref(_layernorm(x, axis=-1), L0_attn_b_wq, L0_attn_b_wk, L0_attn_b_wv, L0_attn_b_wo, L0_attn_b_pope_bias)
    x = x + _L0_ffn_ref(_layernorm(x, axis=-1), L0_ffn_base_w, L0_ffn_base_b, L0_ffn_lora_A, L0_ffn_lora_B, L0_ffn_router_w, L0_ffn_router_b)
    x = x + _L1_attn_a_ref(_layernorm(x, axis=-1), L1_attn_a_W_k, L1_attn_a_W_v, L1_attn_a_W_o)
    x = x + _L1_ffn_ref(_layernorm(x, axis=-1), L1_ffn_fast_b, L1_ffn_w_fc, L1_ffn_w_proj, L1_ffn_u, L1_ffn_v, L1_ffn_gate)
    x = x + _L1_attn_b_ref(_layernorm(x, axis=-1), L1_attn_b_wq, L1_attn_b_bq, L1_attn_b_wk, L1_attn_b_bk, L1_attn_b_wv, L1_attn_b_bv, L1_attn_b_wo, L1_attn_b_bo, L1_attn_b_wfq, L1_attn_b_bfq, L1_attn_b_wfg, L1_attn_b_bfg, L1_attn_b_up, L1_attn_b_uz)
    x = x + _L1_ffn_ref(_layernorm(x, axis=-1), L1_ffn_fast_b, L1_ffn_w_fc, L1_ffn_w_proj, L1_ffn_u, L1_ffn_v, L1_ffn_gate)
    return x

_drawn_inputs = setup_inputs


def setup_inputs(seed=0):
    import zlib

    import numpy as np

    out = dict(_drawn_inputs(seed))
    spreads = {'L0_attn_a_sk_b2': (0.0, 2.0),
     'L0_attn_a_sv_b2': (0.0, 2.0),
     'L0_attn_a_gnorm_w': (1.0, 0.6),
     'L0_ffn_base_b': (0.0, 0.1),
     'L0_ffn_router_b': (0.0, 0.382)}
    factors = {'L0_attn_a_Wq': 64.0,
     'L0_attn_a_Wk': 64.0,
     'L0_attn_a_sk_w1': 64.0,
     'L0_attn_a_sk_w2': 64.0,
     'L0_attn_a_sv_w1': 28.273,
     'L0_attn_a_sv_w2': 37.007,
     'L1_attn_b_wq': 8.0,
     'L1_attn_b_bq': 28.272,
     'L1_attn_b_wk': 8.0,
     'L1_attn_b_bk': 64.0,
     'L1_attn_b_wv': 5.432,
     'L1_attn_b_bv': 8.0,
     'L1_attn_b_wo': 4.832,
     'L1_attn_b_bo': 11.524,
     'L1_attn_b_wfq': 23.902,
     'L1_attn_b_bfq': 64.0,
     'L1_attn_b_wfg': 36.497,
     'L1_attn_b_bfg': 64.0,
     'L1_attn_b_up': 24.865,
     'L1_attn_b_uz': 48.645,
     'L1_ffn_fast_b': 8.0,
     'L1_ffn_w_fc': 3.318,
     'L1_ffn_w_proj': 2.705,
     'L1_ffn_u': 8.0,
     'L1_ffn_v': 8.0}
    for name, (base, spread) in spreads.items():
        noise = np.random.default_rng([zlib.crc32(name.encode()), seed]).standard_normal(out[name].shape)
        drawn = base * np.exp(spread * noise) if base else spread * noise
        out[name] = jnp.asarray(drawn.astype(out[name].dtype))
    for name, factor in factors.items():
        out[name] = (out[name] * factor).astype(out[name].dtype)
    return out
```

```python
from collections import namedtuple

import numpy as np

import concourse.bass as bass
from concourse import mybir

F32 = mybir.dt.float32
BF16 = mybir.dt.bfloat16
ALU = mybir.AluOpType
ACT = mybir.ActivationFunctionType
AX = mybir.AxisListType

P = 128
NB = 8
T = 512
NT = T // P
D = 128
H = 16
DH = D // H
GH = 4
NG = H // GH
GW = GH * DH
SH = 4
SD = D // SH
SM = 64
LOW = 16
E = 8
R = 16
HID = 512
NK = HID // P
EPS = 1e-5
CLAMP = 32.0


def wait_ge(eng, sem, value):
    if isinstance(value, int) and value <= 0:
        return
    eng.wait_ge(sem, value)


class Shared:
    pass


def wait_alone(eng, sv, *waits):
    for sem, value in waits:
        wait_ge(eng, sem, value)
    if not all(isinstance(value, int) for _, value in waits):
        eng.sem_inc(sv.past, 1)


def skewed(eng, front, back, third=None):
    front(0, 0)
    with eng.Fori(0, NB // 2 - 1) as i:
        front(2 * i + 1, 1)
        back(2 * i, 0)
        front(2 * i + 2, 0)
        back(2 * i + 1, 1)
    front(NB - 1, 1)
    back(NB - 2, 0)
    back(NB - 1, 1)


def over(ap, *shape):
    while len(ap.shape) < len(shape):
        ap = ap.unsqueeze(len(ap.shape))
    return ap.to_broadcast(list(shape))


def tiles_of(b):
    return bass.ds(b * NT, NT)


class NormFront:

    def __init__(self, nc, sv, wo=None, bo=None):
        self.nc, self.sv, self.wo, self.bo = nc, sv, wo, bo
        sb, ps, sem = nc.alloc_sbuf_tensor, nc.alloc_psum_tensor, nc.alloc_semaphore
        n = sv.tag
        self.stats = sb(f"{n}_stats", [P, 2, NT, 6], F32)
        self.meanvar = sb(f"{n}_meanvar", [P, 2, NT, 2], F32)
        self.vareps = sb(f"{n}_vareps", [P, 2, NT], F32)
        self.rstd = sb(f"{n}_rstd", [P, 2, NT], F32)
        self.xn = sb(f"{n}_xn", [P, 2, NT, D], F32)
        self.xnT = [sb(f"{n}_xnT{u}", [P, T], F32) for u in range(2)]
        self.ps_xn = ps(f"{n}_ps_xn", [P, 512], F32)
        self.bn_done = sem(f"{n}_bn_done")
        self.mv_ready = sem(f"{n}_mv_ready")
        self.ve_ready = sem(f"{n}_ve_ready")
        self.rs_ready = sem(f"{n}_rs_ready")
        self.xn_ready = sem(f"{n}_xn_ready")
        self.xn_turned = sem(f"{n}_xn_turned")
        self.xnT_ready = sem(f"{n}_xnT_ready")
        self.xnT_used, self.uses = None, 1
        if wo is not None:
            self.ctx_in = [sb(f"{n}_ctx_in{u}", [P, NT, D], F32) for u in range(2)]
            self.ctxT = [sb(f"{n}_ctxT{u}", [P, T], F32) for u in range(2)]
            self.ps_ctx = ps(f"{n}_ps_ctx", [P, 512], F32)
            self.ps_out = ps(f"{n}_ps_out", [P, 512], F32)
            self.ctx_copied = sem(f"{n}_ctx_copied")
            self.ctx_turned = sem(f"{n}_ctx_turned")
            self.ctxT_ready = sem(f"{n}_ctxT_ready")
            self.out_done = sem(f"{n}_out_done")
            self.res_done = sem(f"{n}_res_done")

    def pool(self, eng, b, u):
        sv = self.sv
        if self.wo is not None:
            wait_ge(eng, self.ctx_turned, b - 1)
            eng.tensor_copy(self.ctx_in[u][:, :, :], sv.ctx[:, tiles_of(b), :]).then_inc(self.ctx_copied, 1)
        wait_alone(eng, sv, (self.mv_ready, b + 1))
        eng.tensor_scalar(self.vareps[:, u, :], self.meanvar[:, u, :, 1], EPS, None, ALU.add).then_inc(self.ve_ready, 1)
        eng.wait_ge(self.ve_ready, b + 1)
        eng.tensor_tensor(self.rstd[:, u, :], self.vareps[:, u, :], sv.minus_half[:, 0:NT], ALU.pow).then_inc(self.rs_ready, 1)

    def tensor(self, eng, b, u):
        sv = self.sv
        if self.wo is not None:
            eng.wait_ge(self.ctx_copied, b + 1)
            wait_ge(eng, self.ctxT_ready, b)
            for t in range(NT):
                last = eng.transpose(self.ps_ctx[:, t * P:(t + 1) * P], self.ctx_in[u][:, t, :], sv.ident[:, :])
            last.then_inc(self.ctx_turned, 1)
            eng.wait_ge(self.ctxT_ready, b + 1)
            wait_ge(eng, self.res_done, b)
            for t in range(NT):
                last = eng.matmul(self.ps_out[:, t * D:(t + 1) * D], self.ctxT[u][:, t * P:(t + 1) * P], self.wo,
                                  start=True, stop=True)
            last.then_inc(self.out_done, 1)
        eng.wait_ge(self.xn_ready, b + 1)
        wait_ge(eng, self.xnT_ready, b)
        for t in range(NT):
            last = eng.transpose(self.ps_xn[:, t * P:(t + 1) * P], self.xn[:, u, t, :], sv.ident[:, :])
        last.then_inc(self.xn_turned, 1)

    def scalar(self, eng, b, u):
        if self.wo is not None:
            eng.wait_ge(self.ctx_turned, b + 1)
            wait_ge(eng, self.out_done, b - 1)
            eng.activation(self.ctxT[u][:, :], self.ps_ctx[:, :], ACT.Copy).then_inc(self.ctxT_ready, 1)
        eng.wait_ge(self.xn_turned, b + 1)
        wait_ge(eng, self.xnT_used, (b - 1) * self.uses)
        eng.activation(self.xnT[u][:, :], self.ps_xn[:, :], ACT.Copy).then_inc(self.xnT_ready, 1)

    def vector(self, eng, b, u):
        sv = self.sv
        x = sv.x[:, tiles_of(b), :]
        if self.wo is not None:
            eng.wait_ge(self.out_done, b + 1)
            out = self.ps_out[:, :].rearrange("p (t d) -> p t d", t=NT)
            eng.tensor_tensor(x, out, x, ALU.add).then_inc(self.res_done, 1)
            wait_alone(eng, sv, (self.res_done, b + 1))
        for t in range(NT):
            last = eng.bn_stats(self.stats[:, u, t, :], sv.x[:, bass.ds(b * NT + t, 1), :].rearrange("p o d -> p (o d)"))
        last.then_inc(self.bn_done, 1)
        wait_alone(eng, sv, (self.bn_done, b + 1))
        for t in range(NT):
            last = eng.bn_aggr(self.meanvar[:, u, t, :], self.stats[:, u, t, :])
        last.then_inc(self.mv_ready, 1)
        eng.wait_ge(self.rs_ready, b + 1)
        wait_ge(eng, self.xn_turned, b - 1)
        for t in range(NT):
            last = eng.tensor_scalar(self.xn[:, u, t, :], sv.x[:, bass.ds(b * NT + t, 1), :].rearrange("p o d -> p (o d)"),
                                     self.meanvar[:, u, t, 0:1], self.rstd[:, u, t:t + 1], ALU.subtract, ALU.mult)
        last.then_inc(self.xn_ready, 1)


def load_phase(nc, sv, a):
    sv.tag = "w"
    with nc.cleanup_on_exit():
        sb, sem = nc.alloc_sbuf_tensor, nc.alloc_semaphore
        square_names = ["L0_attn_b_wq", "L0_attn_b_wk", "L0_attn_b_wv", "L0_attn_b_wo",
                        "L1_attn_a_W_k", "L1_attn_a_W_v", "L1_attn_a_W_o", "L0_ffn_base_w"]
        NS = len(square_names)
        square_raw = sb("square_raw", [P, NS, D], F32)
        router_raw = sb("router_raw", [E, D], F32)
        fc_raw = sb("fc_raw", [P, NK, D], F32)
        proj_raw = sb("proj_raw", [P, HID], F32)
        u_raw = sb("u_raw", [P, NK, R], F32)
        v_raw = sb("v_raw", [R, D], F32)
        fast_raw = sb("fast_raw", [R, R], F32)
        rows = sb("rows", [1, 8 * 256], F32)
        row_at = {"L0_ffn_router_b": (0, E), "L0_ffn_base_b": (128, D), "L1_attn_b_bv": (256, D),
                  "L1_attn_b_bo": (384, D), "L0_attn_a_gnorm_w": (512, SD), "L1_ffn_gate": (576, 1)}
        ones_row = sb("ones_row", [1, P], F32)
        wT = sb("wT", [P, NS, D], F32)
        uT = sb("uT", [R, HID], F32)
        fastT = sb("fastT", [R, R], F32)
        a1T = sb("a1T", [R, D], F32)
        mT = sb("mT", [P, D], F32)
        fc_scale = sb("fc_scale", [P, 4, NK], F32)
        proj_scale = sb("proj_scale", [P, 4], F32)
        fc_eff = sb("fc_eff", [P, NK, D], F32)
        proj_eff = sb("proj_eff", [P, HID], F32)
        fc_pos = sb("fc_pos", [P, NK, D], F32)
        fc_neg = sb("fc_neg", [P, NK, D], F32)
        proj_pos = sb("proj_pos", [P, HID], F32)
        proj_neg = sb("proj_neg", [P, HID], F32)
        bias2 = sb("bias2", [P, 4], F32)
        lowrank = sb("lowrank", [P, HID], F32)
        ps = [nc.alloc_psum_tensor(f"w_ps{i}", [P, 512], F32) for i in range(8)]
        loaded = sem("w_loaded")
        ready = sem("w_memsets")
        turned = sem("w_turned")
        evacuated = sem("w_evacuated")
        step = sem("w_vector_step")

        loads = []

        def load(dst, src):
            loads.append((dst, src))

        load(sv.ident[:, :], a["c_ident"])
        for i, name in enumerate(square_names):
            load(square_raw[:, i, :], a[name])
        load(fc_raw[:, :, :], a["L1_ffn_w_fc"].rearrange("(k p) c -> p k c", p=P))
        load(proj_raw[:, :], a["L1_ffn_w_proj"])
        load(u_raw[:, :, :], a["L1_ffn_u"].rearrange("(k p) r -> p k r", p=P))
        load(v_raw[:, :], a["L1_ffn_v"])
        load(fast_raw[:, :], a["L1_ffn_fast_b"])
        load(router_raw[:, :], a["L0_ffn_router_w"])
        for name, (at, n) in row_at.items():
            load(rows[0:1, at:at + n], a[name].rearrange("(o n) -> o n", o=1))
        load(sv.ffn0_w[:, D:D + E * R].rearrange("p (e r) -> p e r", e=E), a["L0_ffn_lora_A"].rearrange("e d r -> d e r"))
        load(sv.lora_b[:, :], a["L0_ffn_lora_B"].rearrange("e r o -> (e r) o"))
        for b in range(NB):
            load(sv.x[:, b * NT:(b + 1) * NT, :], a["L0_attn_a_hidden_states"][b].rearrange("(t p) d -> p t d", p=P))
        load(sv.block_mask[:, :], a["c_block_mask"])
        load(sv.head_ind[:, :], a["c_head_ind"])
        load(sv.causal[:, :], a["c_causal"])
        load(sv.slot_mask[:, :], a["c_slot_mask"])
        load(sv.positions[:, :], a["c_positions"])
        load(sv.rope[:, :, :], a["c_rope"])
        load(sv.pope_table[:, :, :], a["c_pope"])
        for i, n in enumerate(("Wq", "Wk", "Wv", "Wg")):
            load(sv.slot_w[:, i * D:(i + 1) * D], a["L0_attn_a_" + n])
        load(sv.slot_wo[:, :], a["L0_attn_a_Wo"])
        load(sv.slot_w1[:, 0:LOW], a["L0_attn_a_sk_w1"])
        load(sv.slot_w1[:, LOW:2 * LOW], a["L0_attn_a_sv_w1"])
        for i, n in enumerate(("wq", "wk", "wv", "wo", "wfq", "wfg")):
            load(sv.l1b_w[:, i, :], a["L1_attn_b_" + n])
        for i, n in enumerate(("bq", "bk", "bfq", "bfg")):
            load(sv.l1b_b[:, i:i + 1], a["L1_attn_b_" + n].rearrange("(p o) -> p o", o=1))
        load(sv.l1b_u[:, 0:1], a["L1_attn_b_up"].rearrange("h o d -> (h d) o"))
        load(sv.l1b_u[:, 1:2], a["L1_attn_b_uz"].rearrange("h o d -> (h d) o"))
        load(sv.pope_bias[:, 0:1], a["L0_attn_b_pope_bias"].rearrange("h (d o) -> (h d) o", o=1))
        after_memset = len(loads)
        load(sv.slot_w2[0:LOW, 0:SH * SM], a["L0_attn_a_sk_w2"])
        load(sv.slot_w2[LOW:2 * LOW, SH * SM:], a["L0_attn_a_sv_w2"])
        load(sv.slot_w2[2 * LOW:2 * LOW + 1, 0:SH * SM], a["L0_attn_a_sk_b2"].rearrange("(o n) -> o n", o=1))
        load(sv.slot_w2[2 * LOW:2 * LOW + 1, SH * SM:], a["L0_attn_a_sv_b2"].rearrange("(o n) -> o n", o=1))
        all_loaded = 16 * len(loads)

        with nc.Block() as block:
            @block.sync
            def _(sp):
                for i, (dst, src) in enumerate(loads):
                    if i == after_memset:
                        sp.wait_ge(ready, 2)
                    sp.dma_start(dst, src).then_inc(loaded, 16)
                sp.wait_ge(loaded, all_loaded)

            @block.gpsimd
            def _(pool):
                pool.memset(ones_row[:, :], 1.0).then_inc(ready, 1)
                pool.memset(sv.slot_w2[:, :], 0.0).then_inc(ready, 1)
                pool.memset(sv.minus_half[:, :], -0.5).then_inc(ready, 1)
                pool.memset(sv.ones[:, :], 1.0).then_inc(ready, 1)
                pool.wait_ge(loaded, all_loaded)
                pool.tensor_copy(sv.ident_bf[:, :], sv.ident[:, :])

            @block.tensor
            def _(pe):
                pe.wait_ge(loaded, all_loaded)
                pe.wait_ge(ready, 1)
                for i in range(NS):
                    last = pe.transpose(ps[i // 4][:, (i % 4) * D:(i % 4 + 1) * D], square_raw[:, i, :], sv.ident[:, :])
                pe.transpose(ps[2][:, 0:E], router_raw[:, :], sv.ident[0:E, 0:E])
                last = pe.transpose(ps[2][0:R, 128:128 + R], fast_raw[:, :], sv.ident[0:R, 0:R])
                for k in range(NK):
                    last = pe.transpose(ps[3][0:R, k * P:(k + 1) * P], u_raw[:, k, :], sv.ident[:, :])
                for name, (at, n) in row_at.items():
                    c = 0 if name == "L1_ffn_gate" else at % 512
                    to = ps[4] if at < 512 else ps[5]
                    if name == "L1_ffn_gate":
                        c = 64
                    last = pe.matmul(to[:, c:c + n], ones_row[:, :], rows[0:1, at:at + n], start=True, stop=True)
                last.then_inc(turned, 1)
                pe.wait_ge(evacuated, 1)
                pe.matmul(ps[6][0:R, 0:D], fastT[:, :], v_raw[:, :], start=True, stop=True)
                last = pe.matmul(ps[7][:, 0:D], wT[:, 5, :], wT[:, 4, :], start=True, stop=True)
                last.then_inc(turned, 1)
                pe.wait_ge(evacuated, 2)
                pe.matmul(ps[0][:, :], a1T[:, :], uT[:, :], start=True, stop=True)
                last = pe.matmul(ps[1][:, 0:D], mT[:, :], wT[:, 6, :], start=True, stop=True)
                last.then_inc(turned, 1)
                pe.wait_ge(evacuated, 3)
                for k in range(NK):
                    pe.transpose(ps[2][:, k * P:(k + 1) * P], fc_eff[:, k, :], sv.ident[:, :])
                for k in range(NK):
                    last = pe.transpose(ps[3][:, k * P:(k + 1) * P], proj_eff[:, k * P:(k + 1) * P], sv.ident[:, :])
                last.then_inc(turned, 1)

            @block.vector
            def _(dve):
                steps = [0]

                def then_wait(instruction):
                    steps[0] += 1
                    instruction.then_inc(step, 1)
                    dve.wait_ge(step, steps[0])

                dve.wait_ge(turned, 1)
                dve.tensor_copy(wT[:, 0:4, :], ps[0][:, :].rearrange("p (n d) -> p n d", n=4))
                dve.tensor_copy(wT[:, 4:8, :], ps[1][:, :].rearrange("p (n d) -> p n d", n=4))
                dve.tensor_copy(sv.ffn0_w[:, D + E * R:D + E * R + E], ps[2][:, 0:E])
                dve.tensor_copy(fastT[:, :], ps[2][0:R, 128:128 + R])
                dve.tensor_copy(uT[:, :], ps[3][0:R, :])
                dve.tensor_copy(sv.router_bias[:, :], ps[4][:, 0:E])
                dve.tensor_copy(sv.base_bias[:, :], ps[4][:, 128:256])
                dve.tensor_copy(sv.bv[:, :], ps[4][:, 256:384])
                dve.tensor_copy(sv.bo[:, :], ps[4][:, 384:512])
                dve.tensor_copy(sv.gnorm[:, :], ps[5][:, 0:SD])
                dve.tensor_copy(sv.gate[:, :], ps[5][:, 64:65]).then_inc(evacuated, 1)
                dve.wait_ge(evacuated, 1)
                dve.tensor_copy(sv.l0b_w[:, :, :], wT[:, 0:4, :])
                dve.tensor_copy(sv.l1a_wk[:, :], wT[:, 4, :])
                dve.tensor_copy(sv.ffn0_w[:, 0:D], wT[:, 7, :])
                dve.wait_ge(turned, 2)
                dve.tensor_copy(a1T[:, :], ps[6][0:R, 0:D])
                dve.tensor_tensor(mT[:, :], ps[7][:, 0:D], sv.block_mask[:, :], ALU.mult).then_inc(evacuated, 1)
                dve.wait_ge(turned, 3)
                dve.tensor_copy(sv.l1a_wo[:, :], ps[1][:, 0:D])
                then_wait(dve.tensor_scalar(lowrank[:, :], ps[0][:, :], sv.gate[:, 0:1], None, ALU.mult))

                def ternary(raw, eff, pos, neg, scale, n, parts):
                    view = raw if parts > 1 else raw.unsqueeze(1)
                    then_wait(dve.tensor_reduce(scale[0], view, AX.X, ALU.add, apply_absolute_value=True))
                    then_wait(dve.tensor_scalar(scale[1], scale[0], 1.0 / n, 1e-5, ALU.mult, ALU.max))
                    dve.tensor_scalar(scale[2], scale[1], 0.5, None, ALU.mult)
                    then_wait(dve.tensor_scalar(scale[3], scale[1], -0.5, None, ALU.mult))
                    for k in range(parts):
                        w, o = (raw[:, k, :], slice(None)) if parts > 1 else (raw, None)
                        p_, n_ = (pos[:, k, :], neg[:, k, :]) if parts > 1 else (pos, neg)
                        dve.tensor_scalar(p_, w, scale[2][:, k:k + 1], None, ALU.is_gt)
                        last = dve.tensor_scalar(n_, w, scale[3][:, k:k + 1], None, ALU.is_lt)
                    then_wait(last)
                    then_wait(dve.tensor_tensor(pos, pos, neg, ALU.subtract))
                    then_wait(dve.tensor_tensor(pos, pos, raw, ALU.subtract))
                    then_wait(dve.tensor_tensor(pos, pos, raw, ALU.add))
                    for k in range(parts):
                        e_, p_ = (eff[:, k, :], pos[:, k, :]) if parts > 1 else (eff, pos)
                        last = dve.tensor_scalar(e_, p_, scale[1][:, k:k + 1], None, ALU.mult)
                    return last

                ternary(fc_raw[:, :, :], fc_eff[:, :, :], fc_pos[:, :, :], fc_neg[:, :, :],
                        [fc_scale[:, i, :] for i in range(4)], D, NK)
                ternary(proj_raw[:, :], proj_eff[:, :], proj_pos[:, :], proj_neg[:, :],
                        [proj_scale[:, i:i + 1] for i in range(4)], HID, 1).then_inc(evacuated, 1)
                dve.wait_ge(turned, 4)
                dve.tensor_tensor(sv.ffn1_fc[:, :], ps[2][:, :], lowrank[:, :], ALU.add)
                dve.tensor_copy(sv.ffn1_proj[:, :, :], ps[3][:, :].rearrange("p (k d) -> p k d", k=NK))
                for i in range(2):
                    dve.tensor_scalar(sv.l1b_up[:, i * H:(i + 1) * H], sv.head_ind[:, :], sv.l1b_u[:, i:i + 1], None, ALU.mult)


def ffn0_phase(nc, sv, tag, wo=None):
    sv.tag = tag
    NW = D + E * R + E
    with nc.cleanup_on_exit():
        sb = nc.alloc_sbuf_tensor

        def sem(name):
            return nc.alloc_semaphore(f"{tag}_{name}")

        front = NormFront(nc, sv, wo)
        logits = sb(f"{tag}_logits", [P, NT, E], F32)
        top = sb(f"{tag}_top", [P, NT, 8], F32)
        less = sb(f"{tag}_less", [P, NT, E], F32)
        keep = sb(f"{tag}_keep", [P, NT, E], F32)
        expd = sb(f"{tag}_expd", [P, NT, E], F32)
        kept = sb(f"{tag}_kept", [P, NT, E], F32)
        total = sb(f"{tag}_total", [P, NT], F32)
        inv = sb(f"{tag}_inv", [P, NT], F32)
        weight = sb(f"{tag}_weight", [P, NT, E], F32)
        axw = sb(f"{tag}_axw", [P, NT, E * R], F32)
        axwT = sb(f"{tag}_axwT", [P, T], F32)
        tok = nc.alloc_psum_tensor(f"{tag}_tok", [P, NT, 512], F32)
        ps_ax = nc.alloc_psum_tensor(f"{tag}_ps_ax", [P, 512], F32)
        tok_done, logits_ready, less_ready, exp_ready = sem("tok_done"), sem("logits_ready"), sem("less_ready"), sem("exp_ready")
        top_ready, kept_ready, total_ready, inv_ready = sem("top_ready"), sem("kept_ready"), sem("total_ready"), sem("inv_ready")
        weight_ready, axw_ready, ax_turned, axT_ready = sem("weight_ready"), sem("axw_ready"), sem("ax_turned"), sem("axT_ready")
        out_done, bias_added, x_done = sem("lora_done"), sem("bias_added"), sem("x_done")
        front.xnT_used = tok_done

        with nc.Block() as block:
            @block.gpsimd
            def _(pool):
                def back(b, u):
                    pool.wait_ge(front.xn_ready, b + 1)
                    x = sv.x[:, tiles_of(b), :]
                    pool.tensor_tensor(x, x, sv.base_bias[:, :].unsqueeze(1).to_broadcast([P, NT, D]), ALU.add).then_inc(bias_added, 1)
                skewed(pool, lambda b, u: front.pool(pool, b, u), back)

            @block.tensor
            def _(pe):
                def back(b, u):
                    pe.wait_ge(front.xnT_ready, b + 1)
                    wait_ge(pe, x_done, b)
                    for t in range(NT):
                        last = pe.matmul(tok[:, t, 0:NW], front.xnT[u][:, t * P:(t + 1) * P], sv.ffn0_w[:, :],
                                         start=True, stop=False, skip_group_check=True)
                    last.then_inc(tok_done, 1)
                    pe.wait_ge(axw_ready, b + 1)
                    wait_ge(pe, axT_ready, b)
                    for t in range(NT):
                        last = pe.transpose(ps_ax[:, t * P:(t + 1) * P], axw[:, t, :], sv.ident[:, :])
                    last.then_inc(ax_turned, 1)
                    pe.wait_ge(axT_ready, b + 1)
                    for t in range(NT):
                        last = pe.matmul(tok[:, t, 0:D], axwT[:, t * P:(t + 1) * P], sv.lora_b[:, :],
                                         start=False, stop=True, skip_group_check=True)
                    last.then_inc(out_done, 1)
                skewed(pe, lambda b, u: front.tensor(pe, b, u), back)

            @block.scalar
            def _(act):
                def back(b, u):
                    act.wait_ge(less_ready, b + 1)
                    wait_ge(act, kept_ready, b)
                    act.activation(expd[:, :, :], less[:, :, :], ACT.Exp).then_inc(exp_ready, 1)
                    act.wait_ge(ax_turned, b + 1)
                    wait_ge(act, out_done, b)
                    act.activation(axwT[:, :], ps_ax[:, :], ACT.Copy).then_inc(axT_ready, 1)
                skewed(act, lambda b, u: front.scalar(act, b, u), back)

            @block.vector
            def _(dve):
                def back(b, u):
                    dve.wait_ge(tok_done, b + 1)
                    dve.tensor_tensor(logits[:, :, :], tok[:, :, D + E * R:NW], sv.router_bias[:, :].unsqueeze(1).to_broadcast([P, NT, E]),
                                      ALU.add).then_inc(logits_ready, 1)
                    wait_alone(dve, sv, (logits_ready, b + 1))
                    for t in range(NT):
                        last = dve.max(top[:, t, :], logits[:, t, :])
                    last.then_inc(top_ready, 1)
                    dve.wait_ge(top_ready, b + 1)
                    dve.tensor_tensor(keep[:, :, :], logits[:, :, :], over(top[:, :, 1], P, NT, E), ALU.is_ge)
                    wait_ge(dve, exp_ready, b)
                    dve.tensor_tensor(less[:, :, :], logits[:, :, :], over(top[:, :, 0], P, NT, E), ALU.subtract).then_inc(less_ready, 1)
                    dve.wait_ge(exp_ready, b + 1)
                    dve.tensor_tensor(kept[:, :, :], expd[:, :, :], keep[:, :, :], ALU.mult).then_inc(kept_ready, 1)
                    dve.wait_ge(kept_ready, b + 1)
                    dve.tensor_reduce(total[:, :], kept[:, :, :], AX.X, ALU.add).then_inc(total_ready, 1)
                    dve.wait_ge(total_ready, b + 1)
                    dve.reciprocal(inv[:, :], total[:, :]).then_inc(inv_ready, 1)
                    dve.wait_ge(inv_ready, b + 1)
                    dve.scalar_tensor_tensor(out=weight[:, :, :], in0=kept[:, :, :], scalar=2.0, in1=over(inv[:, :], P, NT, E),
                                             op0=ALU.mult, op1=ALU.mult).then_inc(weight_ready, 1)
                    dve.wait_ge(weight_ready, b + 1)
                    wait_ge(dve, ax_turned, b)
                    for t in range(NT):
                        last = dve.tensor_tensor(axw[:, t, :].rearrange("p (e r) -> p e r", e=E),
                                                 tok[:, t, D:D + E * R].rearrange("p (e r) -> p e r", e=E),
                                                 over(weight[:, t, :], P, E, R), ALU.mult)
                    last.then_inc(axw_ready, 1)
                    dve.wait_ge(out_done, b + 1)
                    dve.wait_ge(bias_added, b + 1)
                    x = sv.x[:, tiles_of(b), :]
                    dve.tensor_tensor(x, tok[:, :, 0:D], x, ALU.add).then_inc(x_done, 1)
                skewed(dve, lambda b, u: front.vector(dve, b, u), back)
        return


def ffn1_phase(nc, sv, tag, wo=None, bo=None, out=None):
    sv.tag = tag
    with nc.cleanup_on_exit():
        sb = nc.alloc_sbuf_tensor

        def sem(name):
            return nc.alloc_semaphore(f"{tag}_{name}")

        front = NormFront(nc, sv, wo)
        r = [sb(f"{tag}_r{k}", [P, T], F32) for k in range(NK)]
        r2 = [sb(f"{tag}_r2{k}", [P, T], F32) for k in range(NK)]
        ps_h = nc.alloc_psum_tensor(f"{tag}_ps_h", [P, NK, 512], F32)
        ps_o = nc.alloc_psum_tensor(f"{tag}_ps_o", [P, 512], F32)
        h_done, relu_done, sq_done = sem("h_done"), sem("relu_done"), [sem(f"sq_done{k % 2}") for k in range(2)]
        o_done, x_done, stored = sem("o_done"), sem("x_done"), sem("stored")
        bo_done = sem("bo_done")
        front.xnT_used, front.uses = h_done, NK

        with nc.Block() as block:
            @block.gpsimd
            def _(pool):
                def ahead(b, u):
                    if bo is not None:
                        x = sv.x[:, tiles_of(b), :]
                        pool.tensor_tensor(x, x, bo.unsqueeze(1).to_broadcast([P, NT, D]), ALU.add).then_inc(bo_done, 1)
                    front.pool(pool, b, u)

                def back(b, u):
                    for k in (1, 3):
                        pool.wait_ge(relu_done, b * NK + k + 1)
                        wait_ge(pool, o_done, b)
                        pool.tensor_tensor(r2[k][:, :], r[k][:, :], r[k][:, :], ALU.mult).then_inc(sq_done[1], 1)
                skewed(pool, ahead, back)

            @block.tensor
            def _(pe):
                def back(b, u):
                    pe.wait_ge(front.xnT_ready, b + 1)
                    for k in range(NK):
                        wait_ge(pe, relu_done, b * NK)
                        pe.matmul(ps_h[:, k, :], sv.ffn1_fc[:, k * P:(k + 1) * P], front.xnT[u][:, :],
                                  start=True, stop=True).then_inc(h_done, 1)
                    pe.wait_ge(sq_done[0], 2 * b + 2)
                    pe.wait_ge(sq_done[1], 2 * b + 2)
                    wait_ge(pe, x_done, b)
                    for t in range(NT):
                        for k in range(NK):
                            last = pe.matmul(ps_o[:, t * D:(t + 1) * D], r2[k][:, t * P:(t + 1) * P], sv.ffn1_proj[:, k, :],
                                             start=(k == 0), stop=(k == NK - 1))
                    last.then_inc(o_done, 1)
                skewed(pe, lambda b, u: front.tensor(pe, b, u), back)

            @block.scalar
            def _(act):
                def back(b, u):
                    for k in range(NK):
                        act.wait_ge(h_done, b * NK + k + 1)
                        wait_ge(act, sq_done[k % 2], 2 * b)
                        act.activation(r[k][:, :], ps_h[:, k, :], ACT.Relu).then_inc(relu_done, 1)
                skewed(act, lambda b, u: front.scalar(act, b, u), back)

            @block.vector
            def _(dve):
                def ahead(b, u):
                    if bo is not None:
                        dve.wait_ge(bo_done, b + 1)
                    front.vector(dve, b, u)

                def back(b, u):
                    for k in (0, 2):
                        dve.wait_ge(relu_done, b * NK + k + 1)
                        wait_ge(dve, o_done, b)
                        dve.tensor_tensor(r2[k][:, :], r[k][:, :], r[k][:, :], ALU.mult).then_inc(sq_done[0], 1)
                    dve.wait_ge(o_done, b + 1)
                    x = sv.x[:, tiles_of(b), :]
                    dve.tensor_tensor(x, ps_o[:, :].rearrange("p (t d) -> p t d", t=NT), x, ALU.add).then_inc(x_done, 1)
                skewed(dve, ahead, back)

            if out is not None:
                @block.sync
                def _(sp):
                    with sp.Fori(0, NB) as b:
                        sp.wait_ge(x_done, b + 1)
                        sp.dma_start(out[bass.ds(b, 1), :, :].rearrange("o (t p) d -> p (o t) d", p=P),
                                     sv.x[:, tiles_of(b), :]).then_inc(stored, 16)
                    sp.wait_ge(stored, 16 * NB)


COMBOS = ((0, 0), (0, 1), (0, 2), (1, 0), (1, 1), (2, 0))


def split(eng, src, part, rest, made, b, alone=None):
    eng.tensor_copy(part(0), src).then_inc(made, 1)
    eng.wait_ge(made, 4 * b + 1)
    eng.tensor_tensor(rest, src, part(0), ALU.subtract).then_inc(made, 1)
    wait = wait_ge if alone is None else lambda e, s, v: wait_alone(e, alone, (s, v))
    wait(eng, made, 4 * b + 2)
    eng.tensor_copy(part(1), rest).then_inc(made, 1)
    eng.wait_ge(made, 4 * b + 3)
    eng.tensor_tensor(part(2), rest, part(1), ALU.subtract).then_inc(made, 1)


def l1a_prep_phase(nc, sv, tag):
    sv.tag = tag
    alpha = float(np.sqrt(2.0 * DH ** -0.5))
    with nc.cleanup_on_exit():
        sb = nc.alloc_sbuf_tensor

        def sem(name):
            return nc.alloc_semaphore(f"{tag}_{name}")

        front = NormFront(nc, sv)
        scaled = [sb(f"{tag}_scaled{u}", [P, T], F32) for u in range(2)]
        square = sb(f"{tag}_square", [P, T], F32)
        rest = sb(f"{tag}_rest", [P, T], F32)
        parts = [sb(f"{tag}_parts{u}", [P, 3, T], BF16) for u in range(2)]
        norm = sb(f"{tag}_norm", [H, T], F32)
        nrest = sb(f"{tag}_nrest", [H, T], F32)
        nparts = [sb(f"{tag}_nparts{u}", [H, 3, T], BF16) for u in range(2)]
        ps_q = nc.alloc_psum_tensor(f"{tag}_ps_q", [P, 512], F32)
        ps_v = nc.alloc_psum_tensor(f"{tag}_ps_v", [P, 512], F32)
        ps_n = nc.alloc_psum_tensor(f"{tag}_ps_n", [P, 512], F32)
        q_done, v_done, n_done = sem("q_done"), sem("v_done"), sem("n_done")
        scaled_ready, v_ready, norm_ready, square_ready = sem("scaled_ready"), sem("v_ready"), sem("norm_ready"), sem("square_ready")
        split_steps, nsplit_steps, stored, nstored = sem("split_steps"), sem("nsplit_steps"), sem("stored"), sem("nstored")
        front.xnT_used = v_done

        with nc.Block() as block:
            @block.tensor
            def _(pe):
                def back(b, u):
                    pe.wait_ge(front.xnT_ready, b + 1)
                    wait_ge(pe, scaled_ready, b)
                    pe.matmul(ps_q[:, :], sv.l1a_wk[:, :], front.xnT[u][:, :], start=True, stop=True).then_inc(q_done, 1)
                    wait_ge(pe, v_ready, b)
                    for t in range(NT):
                        last = pe.matmul(ps_v[:, t * D:(t + 1) * D], front.xnT[u][:, t * P:(t + 1) * P], sv.l1a_wk[:, :],
                                         start=True, stop=True)
                    last.then_inc(v_done, 1)
                    pe.wait_ge(square_ready, b + 1)
                    wait_ge(pe, norm_ready, b)
                    pe.matmul(ps_n[0:H, :], sv.head_ind[:, :], square[:, :], start=True, stop=True).then_inc(n_done, 1)
                skewed(pe, lambda b, u: front.tensor(pe, b, u), back)

            @block.scalar
            def _(act):
                def back(b, u):
                    act.wait_ge(q_done, b + 1)
                    wait_ge(act, split_steps, 4 * b)
                    act.activation(scaled[u][:, :], ps_q[:, :], ACT.Copy, scale=alpha).then_inc(scaled_ready, 1)
                    act.wait_ge(v_done, b + 1)
                    act.activation(sv.vtok[:, tiles_of(b), :], ps_v[:, :].rearrange("p (t d) -> p t d", t=NT), ACT.Copy).then_inc(v_ready, 1)
                    act.wait_ge(n_done, b + 1)
                    wait_ge(act, nsplit_steps, 4 * b)
                    act.activation(norm[:, :], ps_n[0:H, :], ACT.Copy, scale=-0.5).then_inc(norm_ready, 1)
                skewed(act, lambda b, u: front.scalar(act, b, u), back)

            @block.vector
            def _(dve):
                def back(b, u):
                    dve.wait_ge(scaled_ready, b + 1)
                    wait_ge(dve, stored, 16 * b)
                    split(dve, scaled[u][:, :], lambda i: parts[u][:, i, :], rest[:, :], split_steps, b)
                skewed(dve, lambda b, u: front.vector(dve, b, u), back)

            @block.gpsimd
            def _(pool):
                def back(b, u):
                    pool.wait_ge(scaled_ready, b + 1)
                    wait_ge(pool, n_done, b)
                    pool.tensor_tensor(square[:, :], scaled[u][:, :], scaled[u][:, :], ALU.mult).then_inc(square_ready, 1)
                    wait_alone(pool, sv, (norm_ready, b + 1), (nstored, 16 * b))
                    split(pool, norm[:, :], lambda i: nparts[u][:, i, :], nrest[:, :], nsplit_steps, b, alone=sv)
                skewed(pool, lambda b, u: front.pool(pool, b, u), back)

            @block.sync
            def _(sp):
                def store(b, u):
                    wait_alone(sp, sv, (split_steps, 4 * b + 4))
                    sp.wait_ge(stored, 16 * b)
                    sp.dma_start(sv.q_parts[bass.ds(b, 1), :, 0, :, :].rearrange("o i r t -> r (o i) t"), parts[u][:, :, :]).then_inc(stored, 16)
                    wait_alone(sp, sv, (nsplit_steps, 4 * b + 4))
                    sp.wait_ge(nstored, 16 * b)
                    sp.dma_start(sv.n_parts[bass.ds(b, 1), :, :, :].rearrange("o i h t -> h (o i) t"), nparts[u][:, :, :]).then_inc(nstored, 16)
                with sp.Fori(0, NB // 2) as i:
                    store(2 * i, 0)
                    store(2 * i + 1, 1)
                sp.wait_ge(stored, 16 * NB)
                sp.wait_ge(nstored, 16 * NB)


def groups(eng, body):
    for g in range(NG):
        body(g, 0, g)
    with eng.Fori(1, NB) as b:
        for g in range(NG):
            body(NG * b + g, b, g)


def attention_phase(nc, sv, tag, rows, loads, ones_from=0, with_max=False):
    sv.tag = tag
    VW = 16
    LAG = 2 if with_max else 0
    NPV = 1 if with_max else 2
    SLOTS = NG
    all_rows = rows + 2 if with_max else rows
    UNITS = 2 * NT
    TILES = GH * NT
    N = NB * NG
    with nc.cleanup_on_exit():
        sb = nc.alloc_sbuf_tensor

        def sem(name):
            return nc.alloc_semaphore(f"{tag}_{name}")

        q_stack = [sb(f"{tag}_q_stack{u}", [all_rows, GH, T], BF16) for u in range(SLOTS)]
        k_stack = [sb(f"{tag}_k_stack{u}", [all_rows, GH, T], BF16) for u in range(SLOTS)]
        v_ones = [sb(f"{tag}_v_ones{u}", [P, NT, GH, VW], F32) for u in range(2)]
        probs = [sb(f"{tag}_probs{c}", [P, GH, T], F32) for c in range(2)]
        ctxT = [sb(f"{tag}_ctxT{u}", [P, T], F32) for u in range(2)]
        inv = sb(f"{tag}_inv", [P, NT, GH], F32)
        minus_max = [sb(f"{tag}_minus_max{u}", [P, TILES], F32) for u in range(2)]
        max_parts = sb(f"{tag}_max_parts", [P, 2, TILES], BF16)
        max_rows = sb(f"{tag}_max_rows", [TILES, 2, P], BF16)
        max_dram = nc.dram_tensor(f"{tag}_max_dram", (2, TILES, P), BF16).ap()
        ps_s = [nc.alloc_psum_tensor(f"{tag}_ps_s{s}", [P, 2, 512], F32) for s in range(2)]
        ps_pv = [nc.alloc_psum_tensor(f"{tag}_ps_pv{u}", [P, 512], F32) for u in range(NPV)]
        ps_t = nc.alloc_psum_tensor(f"{tag}_ps_t", [P, 512], F32)
        ps_m = [nc.alloc_psum_tensor(f"{tag}_ps_m{s}", [P, 512], F32) for s in range(2)] if with_max else []
        prepared, zeroed, loaded = sem("prepared"), sem("zeroed"), [sem(f"loaded{u}") for u in range(SLOTS)]
        scores_done, exp_done, pv_done = sem("scores_done"), sem("exp_done"), sem("pv_done")
        v_copied, ctxT_ready, turned, inv_ready, ctx_ready = sem("v_copied"), sem("ctxT_ready"), sem("turned"), sem("inv_ready"), sem("ctx_ready")
        tile_done, max_done, hi_ready, parts_ready = sem("tile_done"), sem("max_done"), sem("hi_ready"), sem("parts_ready")
        max_turned, rows_ready, rows_stored, rows_loaded = sem("max_turned"), sem("rows_ready"), sem("rows_stored"), sem("rows_loaded")
        LOADS = len(loads(0, 0, q_stack[0], k_stack[0]))

        with nc.Block() as block:
            @block.sync
            def _(sp):
                sp.wait_ge(zeroed, 1)

                def max_to_stack(n, slot):
                    sp.wait_ge(rows_ready, n + 1)
                    sp.dma_start(max_dram.rearrange("i r q -> r i q"), max_rows[:, :, :]).then_inc(rows_stored, 16)
                    sp.wait_ge(rows_stored, 16 * (n + 1))
                    sp.dma_start(q_stack[slot][rows:rows + 2, :, :], max_dram.rearrange("i (h t) q -> i h (t q)", h=GH)).then_inc(rows_loaded, 16)
                    wait_alone(sp, sv, (rows_loaded, 16 * (n + 1)))

                def load(n, b, g):
                    wait_ge(sp, scores_done, UNITS * (n - SLOTS + 1))
                    for src, dst in loads(b, g, q_stack[g], k_stack[g]):
                        sp.dma_start(dst, src).then_inc(loaded[g], 16)
                    if with_max and not (isinstance(n, int) and n < 2):
                        max_to_stack(n - 2, (g - 2) % NG)
                groups(sp, load)
                if with_max:
                    max_to_stack(N - 2, NG - 2)
                    max_to_stack(N - 1, NG - 1)

            @block.gpsimd
            def _(pool):
                for u in range(2):
                    last = pool.memset(v_ones[u][:, :, :, :], 0.0)
                last.then_inc(prepared, 1)
                pool.wait_ge(prepared, 1)
                for u in range(2):
                    last = pool.memset(v_ones[u][:, :, :, DH:DH + 1], 1.0)
                last.then_inc(prepared, 1)
                pool.wait_ge(prepared, 2)

                def copy_v(n, b, g):
                    wait_ge(pool, pv_done, NT * (n - 1))
                    pool.tensor_copy(v_ones[g % 2][:, :, :, 0:DH],
                                     sv.vtok[:, tiles_of(b), g * GW:(g + 1) * GW].rearrange("p t (h d) -> p t h d", h=GH)).then_inc(v_copied, 1)
                groups(pool, copy_v)

            @block.tensor
            def _(pe):
                pe.wait_ge(zeroed, 1)

                def unit(n, g, v):
                    c, pair = divmod(v, 2)
                    wait_ge(pe, exp_done, UNITS * n + v - 1)
                    for j in range(2):
                        h = 2 * pair + j
                        last = pe.matmul(ps_s[v % 2][:, j, :], k_stack[g][:, h, c * P:(c + 1) * P], q_stack[g][:, h, :],
                                         start=True, stop=True)
                    last.then_inc(scores_done, 1)

                def pv(n, g, c):
                    pe.wait_ge(exp_done, UNITS * n + 2 * c + 2)
                    if c == 0:
                        pe.wait_ge(v_copied, n + 1)
                        wait_ge(pe, ctxT_ready, n - NPV + 1)
                    for h in range(GH):
                        last = pe.matmul(ps_pv[g % NPV][32 * h:32 * h + VW, :], v_ones[g % 2][:, c, h, :], probs[c % 2][:, h, :],
                                         start=(c == 0), stop=(c == NT - 1))
                    last.then_inc(pv_done, 1)

                def turn(n, g):
                    pe.wait_ge(ctxT_ready, n + 1)
                    wait_ge(pe, ctx_ready, n)
                    for t in range(NT):
                        last = pe.transpose(ps_t[:, t * P:(t + 1) * P], ctxT[g % 2][:, t * P:(t + 1) * P], sv.ident[:, :])
                    last.then_inc(turned, 1)

                def tile(n, g, k):
                    h, t = divmod(k, NT)
                    wait_ge(pe, max_done, TILES * n + k - 1)
                    if k == 2:
                        wait_ge(pe, rows_ready, n)
                    pe.matmul(ps_m[k % 2][:, :], q_stack[g][0:rows, h, t * P:(t + 1) * P], k_stack[g][0:rows, h, :],
                              start=True, stop=True).then_inc(tile_done, 1)

                def turn_max(n, seen):
                    pe.wait_ge(parts_ready, n + 1)
                    pe.wait_ge(max_done, seen)
                    to = ps_m[0][:, :].bitcast(BF16)
                    for i in range(2):
                        last = pe.transpose(to[0:TILES, i * P:(i + 1) * P], max_parts[:, i, :], sv.ident_bf[:, :])
                    last.then_inc(max_turned, 1)

                def body(n, b, g):
                    early = isinstance(n, int)
                    if with_max:
                        pe.wait_ge(loaded[g], 16 * LOADS * (b + 1))
                        tile(n, g, 0)
                        tile(n, g, 1)
                        if not (early and n == 0):
                            turn_max(n - 1, TILES * n + 1)
                    m, mg = n - LAG, (g - LAG) % NG
                    if with_max and early and m < 0:
                        for k in range(2, TILES):
                            tile(n, g, k)
                        return
                    if with_max:
                        pe.wait_ge(rows_loaded, 16 * (m + 1))
                    else:
                        pe.wait_ge(loaded[g], 16 * LOADS * (b + 1))
                    chunks(m, mg, early and m == 0, lambda k: tile(n, g, k) if with_max else None)

                def chunks(m, mg, first, tile_at):
                    before = (mg - 1) % NG
                    tiles = iter(range(2, TILES))

                    def some(count):
                        for k in [k for _, k in zip(range(count), tiles)]:
                            tile_at(k)
                    for c in range(NT):
                        unit(m, mg, 2 * c)
                        some(1)
                        unit(m, mg, 2 * c + 1)
                        some(1)
                        if c == 2 and not first:
                            turn(m - 1, before)
                        if c > 0:
                            pv(m, mg, c - 1)
                        elif not first:
                            pv(m - 1, before, NT - 1)
                        some(2 if c < 2 or c == 3 else 1)
                    some(TILES)

                groups(pe, body)
                if with_max:
                    turn_max(N - 1, TILES * N)
                    for m in (N - 2, N - 1):
                        pe.wait_ge(rows_loaded, 16 * (m + 1))
                        chunks(m, m % NG, False, lambda k: None)
                pv(N - 1, NG - 1, NT - 1)
                turn(N - 1, NG - 1)

            @block.scalar
            def _(act):
                def evacuate(n, g):
                    act.wait_ge(pv_done, NT * n + NT)
                    wait_ge(act, turned, n - 1)
                    act.activation(ctxT[g % 2][:, :], ps_pv[g % NPV][:, :], ACT.Copy).then_inc(ctxT_ready, 1)

                def body(n, b, g):
                    for v in range(UNITS):
                        c, pair = divmod(v, 2)
                        act.wait_ge(scores_done, UNITS * n + v + 1)
                        if pair == 0:
                            wait_ge(act, pv_done, NT * n + c - 1)
                        act.activation(probs[c % 2][:, 2 * pair:2 * pair + 2, :], ps_s[v % 2][:, :, :], ACT.Exp).then_inc(exp_done, 1)
                        if v == 2 and not (isinstance(n, int) and n == 0):
                            evacuate(n - 1, (g - 1) % NG)
                groups(act, body)
                evacuate(N - 1, NG - 1)

            @block.vector
            def _(dve):
                if with_max:
                    for u in range(SLOTS):
                        dve.memset(k_stack[u][rows:rows + 2, :, :], 1.0)
                if ones_from:
                    for u in range(SLOTS):
                        dve.memset(q_stack[u][ones_from:, :, :], 1.0)
                        dve.memset(k_stack[u][ones_from:, :, :], 1.0)
                for u in range(NPV):
                    last = dve.memset(ps_pv[u][:, :], 0.0)
                last.then_inc(zeroed, 1)

                def normalise(n, b, g):
                    dve.wait_ge(turned, n + 1)
                    raw = ps_t[:, :].rearrange("p (t h c) -> p t h c", t=NT, h=GH)
                    dve.reciprocal(inv[:, :, :], raw[:, :, :, DH]).then_inc(inv_ready, 1)
                    dve.wait_ge(inv_ready, n + 1)
                    dve.tensor_tensor(sv.ctx[:, tiles_of(b), g * GW:(g + 1) * GW].rearrange("p t (h d) -> p t h d", h=GH),
                                      raw[:, :, :, 0:DH], over(inv[:, :, :], P, NT, GH, DH), ALU.mult).then_inc(ctx_ready, 1)

                def evacuate_rows(n):
                    dve.wait_ge(max_turned, n + 1)
                    wait_ge(dve, rows_loaded, 16 * n)
                    dve.tensor_copy(max_rows[:, :, :], ps_m[0][:, :].bitcast(BF16)[0:TILES, 0:2 * P].rearrange("r (i q) -> r i q", i=2))\
                       .then_inc(rows_ready, 1)

                def body(n, b, g):
                    early = isinstance(n, int)
                    for k in range(TILES):
                        dve.wait_ge(tile_done, TILES * n + k + 1)
                        dve.tensor_reduce(minus_max[g % 2][:, k:k + 1], ps_m[k % 2][:, :], AX.X, ALU.max, negate=True).then_inc(max_done, 1)
                        if k == 1 and not (early and n == 0):
                            evacuate_rows(n - 1)
                        if k == 13 and not (early and n < LAG + 1):
                            normalise(n - LAG - 1, b if g == NG - 1 else b - 1, (g - LAG - 1) % NG)
                    dve.wait_ge(max_done, TILES * (n + 1))
                    wait_ge(dve, max_turned, n)
                    dve.tensor_copy(max_parts[:, 0, :], minus_max[g % 2][:, :]).then_inc(hi_ready, 1)
                    dve.wait_ge(hi_ready, n + 1)
                    dve.tensor_tensor(max_parts[:, 1, :], minus_max[g % 2][:, :], max_parts[:, 0, :], ALU.subtract).then_inc(parts_ready, 1)

                if with_max:
                    groups(dve, body)
                    evacuate_rows(N - 1)
                    for n in range(N - LAG - 1, N):
                        normalise(n, n // NG, n % NG)
                else:
                    groups(dve, normalise)


def l1a_loads(sv):
    def loads(b, g, q_stack, k_stack):
        out = []
        at = bass.ds(b, 1)
        for c, (kp, qp) in enumerate(COMBOS):
            for stack, part in ((q_stack, qp), (k_stack, kp)):
                out.append((sv.q_parts[at, part, 0, g * GW:(g + 1) * GW, :].rearrange("o (h d) t -> (o d) h t", h=GH),
                            stack[c * DH:(c + 1) * DH, :, :]))
        r = len(COMBOS) * DH
        norm = sv.n_parts[at, :, g * GH:(g + 1) * GH, :].rearrange("o i h t -> (o i) h t")
        out.append((norm, q_stack[r:r + 3, :, :]))
        out.append((norm, k_stack[r + 3:r + 6, :, :]))
        return out
    return loads


def l0b_prep_phase(nc, sv, tag):
    sv.tag = tag
    pi = 3.1415925
    with nc.cleanup_on_exit():
        sb = nc.alloc_sbuf_tensor

        def sem(name):
            return nc.alloc_semaphore(f"{tag}_{name}")

        front = NormFront(nc, sv)
        angle = sb(f"{tag}_angle", [P, 8], F32)
        k_table = sb(f"{tag}_k_table", [P, 2, T], F32)
        table_rest = sb(f"{tag}_table_rest", [P, 2, T], F32)
        soft = sb(f"{tag}_soft", [P, 2, T], F32)
        mag = sb(f"{tag}_mag", [P, 2, T], F32)
        embed = [sb(f"{tag}_{n}_embed", [P, 2, T], F32) for n in "qk"]
        rest = [sb(f"{tag}_{n}_rest", [P, 2, T], F32) for n in "qk"]
        parts = [[sb(f"{tag}_{n}_parts{u}", [P, 3, 2, T], BF16) for u in range(2)] for n in "qk"]
        ps_qk = nc.alloc_psum_tensor(f"{tag}_ps_qk", [P, 2, 512], F32)
        ps_v = nc.alloc_psum_tensor(f"{tag}_ps_v", [P, 512], F32)
        sines, angles = sem("sines"), sem("angles")
        qk_done, v_done, v_ready, soft_steps = sem("qk_done"), sem("v_done"), sem("v_ready"), sem("soft_steps")
        mag_ready, embed_ready, table_ready = sem("mag_ready"), [sem("q_embed_ready"), sem("k_embed_ready")], sem("table_ready")
        split_steps, stored = [sem("q_split_steps"), sem("k_split_steps")], [sem("q_stored"), sem("k_stored")]
        front.xnT_used = v_done

        with nc.Block() as block:
            @block.tensor
            def _(pe):
                def back(b, u):
                    pe.wait_ge(front.xnT_ready, b + 1)
                    wait_ge(pe, mag_ready, b)
                    for i in range(2):
                        last = pe.matmul(ps_qk[:, i, :], sv.l0b_w[:, i, :], front.xnT[u][:, :], start=True, stop=True)
                    last.then_inc(qk_done, 1)
                    wait_ge(pe, v_ready, b)
                    for t in range(NT):
                        last = pe.matmul(ps_v[:, t * D:(t + 1) * D], front.xnT[u][:, t * P:(t + 1) * P], sv.l0b_w[:, 2, :],
                                         start=True, stop=True)
                    last.then_inc(v_done, 1)
                skewed(pe, lambda b, u: front.tensor(pe, b, u), back)

            @block.scalar
            def _(act):
                act.wait_ge(angles, 1)
                act.activation(angle[:, 4:5], angle[:, 2:3], ACT.Sin)
                act.activation(angle[:, 5:6], angle[:, 3:4], ACT.Sin).then_inc(sines, 1)

                def back(b, u):
                    act.wait_ge(qk_done, b + 1)
                    wait_ge(act, mag_ready, b)
                    act.activation(soft[:, :, :], ps_qk[:, :, :], ACT.Abs).then_inc(soft_steps, 1)
                    act.wait_ge(soft_steps, 3 * b + 1)
                    act.activation(soft[:, :, :], soft[:, :, :], ACT.Exp, scale=-1.0).then_inc(soft_steps, 1)
                    act.wait_ge(soft_steps, 3 * b + 2)
                    act.activation(soft[:, :, :], soft[:, :, :], ACT.Ln, bias=sv.ones[:, 0:1]).then_inc(soft_steps, 1)
                    act.wait_ge(v_done, b + 1)
                    act.activation(sv.vtok[:, tiles_of(b), :], ps_v[:, :].rearrange("p (t d) -> p t d", t=NT), ACT.Copy).then_inc(v_ready, 1)
                skewed(act, lambda b, u: front.scalar(act, b, u), back)

            @block.vector
            def _(dve):
                steps = [0]

                def then_wait(instruction):
                    steps[0] += 1
                    instruction.then_inc(table_ready, 1)
                    dve.wait_ge(table_ready, steps[0])

                then_wait(dve.tensor_scalar(angle[:, 0:1], sv.pope_bias[:, :], -2.0 * float(np.pi), 0.0, ALU.max, ALU.min))
                then_wait(dve.tensor_scalar(angle[:, 1:2], angle[:, 0:1], float(np.pi), None, ALU.add))
                dve.tensor_scalar(angle[:, 2:3], angle[:, 1:2], -pi, pi, ALU.max, ALU.min)
                then_wait(dve.tensor_scalar(angle[:, 3:4], angle[:, 0:1], 0.5, -pi, ALU.mult, ALU.max))
                dve.tensor_scalar(angle[:, 1:2], angle[:, 0:1], 0.5, None, ALU.mult).then_inc(angles, 1)
                dve.wait_ge(sines, 1)
                dve.tensor_scalar(angle[:, 6:7], angle[:, 4:5], -1.0, None, ALU.mult)
                then_wait(dve.tensor_tensor(angle[:, 7:8], angle[:, 5:6], angle[:, 5:6], ALU.mult))
                then_wait(dve.tensor_scalar(angle[:, 7:8], angle[:, 7:8], -2.0, 1.0, ALU.mult, ALU.add))
                dve.tensor_scalar(table_rest[:, 0, :], sv.pope_table[:, 1, :], angle[:, 4:5], None, ALU.mult)
                then_wait(dve.tensor_scalar(table_rest[:, 1, :], sv.pope_table[:, 0, :], angle[:, 6:7], None, ALU.mult))
                then_wait(dve.scalar_tensor_tensor(out=k_table[:, :, :], in0=sv.pope_table[:, :, :], scalar=angle[:, 7:8],
                                                   in1=table_rest[:, :, :], op0=ALU.mult, op1=ALU.add))

                def back(b, u):
                    dve.wait_ge(soft_steps, 3 * b + 3)
                    wait_ge(dve, embed_ready[1], b)
                    dve.scalar_tensor_tensor(out=mag[:, :, :], in0=ps_qk[:, :, :], scalar=0.0, in1=soft[:, :, :],
                                             op0=ALU.max, op1=ALU.add).then_inc(mag_ready, 1)
                    dve.wait_ge(mag_ready, b + 1)
                    dve.scalar_tensor_tensor(out=embed[0][:, :, :], in0=sv.pope_table[:, :, :], scalar=DH ** -0.5,
                                             in1=mag[:, 0, :].unsqueeze(1).to_broadcast([P, 2, T]), op0=ALU.mult, op1=ALU.mult)\
                       .then_inc(embed_ready[0], 1)
                    dve.wait_ge(embed_ready[0], b + 1)
                    wait_ge(dve, stored[0], 16 * b)
                    split(dve, embed[0][:, :, :], lambda i: parts[0][u][:, i, :, :], rest[0][:, :, :], split_steps[0], b)
                skewed(dve, lambda b, u: front.vector(dve, b, u), back)

            @block.gpsimd
            def _(pool):
                pool.wait_ge(table_ready, 6)

                def back(b, u):
                    pool.wait_ge(mag_ready, b + 1)
                    pool.tensor_tensor(embed[1][:, :, :], k_table[:, :, :], mag[:, 1, :].unsqueeze(1).to_broadcast([P, 2, T]), ALU.mult)\
                        .then_inc(embed_ready[1], 1)
                    wait_alone(pool, sv, (embed_ready[1], b + 1), (stored[1], 16 * b))
                    split(pool, embed[1][:, :, :], lambda i: parts[1][u][:, i, :, :], rest[1][:, :, :], split_steps[1], b, alone=sv)
                skewed(pool, lambda b, u: front.pool(pool, b, u), back)

            @block.sync
            def _(sp):
                def store(b, u):
                    for i, to in enumerate((sv.q_parts, sv.k_parts)):
                        wait_alone(sp, sv, (split_steps[i], 4 * b + 4))
                        sp.wait_ge(stored[i], 16 * b)
                        sp.dma_start(to[bass.ds(b, 1)].rearrange("o i c r t -> r (o i c) t"),
                                     parts[i][u][:, :, :, :].rearrange("p i c t -> p (i c) t")).then_inc(stored[i], 16)
                with sp.Fori(0, NB // 2) as i:
                    store(2 * i, 0)
                    store(2 * i + 1, 1)
                for i in range(2):
                    sp.wait_ge(stored[i], 16 * NB)


def l0b_loads(sv):
    def loads(b, g, q_stack, k_stack):
        out = []
        for c, (kp, qp) in enumerate(COMBOS):
            for stack, parts, part in ((q_stack, sv.q_parts, qp), (k_stack, sv.k_parts, kp)):
                for i in range(2):
                    r = (2 * c + i) * DH
                    out.append((parts[bass.ds(b, 1), part, i, g * GW:(g + 1) * GW, :].rearrange("o (h d) t -> (o d) h t", h=GH),
                                stack[r:r + DH, :, :]))
        return out
    return loads


def l1b_prep_phase(nc, sv, tag):
    sv.tag = tag
    with nc.cleanup_on_exit():
        sb = nc.alloc_sbuf_tensor

        def sem(name):
            return nc.alloc_semaphore(f"{tag}_{name}")

        front = NormFront(nc, sv)
        mixed = [sb(f"{tag}_mixed_{n}", [P, T], F32) for n in "qk"]
        scaled_q = sb(f"{tag}_scaled_q", [P, T], F32)
        rest = [sb(f"{tag}_{n}_rest", [P, T], F32) for n in "qk"]
        parts = [[sb(f"{tag}_{n}_parts{u}", [P, 3, T], BF16) for u in range(2)] for n in "qk"]
        glo = sb(f"{tag}_glo", [P, 4], F32)
        cT = sb(f"{tag}_cT", [P, T], F32)
        gates = sb(f"{tag}_gates", [P, NT, 2 * H], F32)
        bias_sum = sb(f"{tag}_bias_sum", [P, 1], F32)
        ps_q, ps_k, ps_v, ps_c, ps_g, ps_p = [nc.alloc_psum_tensor(f"{tag}_ps_{n}", [P, 512], F32) for n in "qkvcgp"]
        names = ("q_done k_done v_done q_ready k_ready scaled_ready v_ready sum_ready mean_ready c_done g_done gb_ready cT_ready "
                 "p_done exp_ready one_ready recip_ready gate_ready bias_ready").split()
        (q_done, k_done, v_done, q_ready, k_ready, scaled_ready, v_ready, sum_ready, mean_ready, c_done, g_done, gb_ready, cT_ready,
         p_done, exp_ready, one_ready, recip_ready, gate_ready, bias_ready) = [sem(n) for n in names]
        split_steps, stored = [sem("q_split_steps"), sem("k_split_steps")], [sem("q_stored"), sem("k_stored")]
        front.xnT_used = v_done

        with nc.Block() as block:
            @block.tensor
            def _(pe):
                def back(b, u):
                    pe.wait_ge(front.xnT_ready, b + 1)
                    wait_ge(pe, q_ready, b)
                    wait_ge(pe, k_ready, b)
                    pe.matmul(ps_q[:, :], sv.l1b_w[:, 0, :], front.xnT[u][:, :], start=True, stop=True).then_inc(q_done, 1)
                    pe.matmul(ps_k[:, :], sv.l1b_w[:, 1, :], front.xnT[u][:, :], start=True, stop=True).then_inc(k_done, 1)
                    wait_ge(pe, v_ready, b)
                    for t in range(NT):
                        last = pe.matmul(ps_v[:, t * D:(t + 1) * D], front.xnT[u][:, t * P:(t + 1) * P], sv.l1b_w[:, 2, :],
                                         start=True, stop=True)
                    last.then_inc(v_done, 1)
                    pe.wait_ge(q_ready, b + 1)
                    wait_ge(pe, cT_ready, b)
                    pe.matmul(ps_c[:, :], sv.l1b_w[:, 4, :], mixed[0][:, :], start=True, stop=True).then_inc(c_done, 1)
                    pe.wait_ge(mean_ready, b + 1)
                    pe.matmul(ps_g[:, 0:1], sv.l1b_w[:, 5, :], glo[:, 1:2], start=True, stop=True).then_inc(g_done, 1)
                    pe.wait_ge(cT_ready, b + 1)
                    wait_ge(pe, exp_ready, b)
                    for t in range(NT):
                        last = pe.matmul(ps_p[:, t * 2 * H:(t + 1) * 2 * H], cT[:, t * P:(t + 1) * P], sv.l1b_up[:, :],
                                         start=True, stop=True)
                    last.then_inc(p_done, 1)
                skewed(pe, lambda b, u: front.tensor(pe, b, u), back)

            @block.scalar
            def _(act):
                def back(b, u):
                    act.wait_ge(q_done, b + 1)
                    wait_ge(act, scaled_ready, b)
                    wait_ge(act, c_done, b)
                    act.activation(mixed[0][:, :], ps_q[:, :], ACT.Identity, bias=sv.l1b_b[:, 0:1]).then_inc(q_ready, 1)
                    act.wait_ge(k_done, b + 1)
                    wait_ge(act, split_steps[1], 4 * b)
                    act.activation(mixed[1][:, :], ps_k[:, :], ACT.Identity, bias=sv.l1b_b[:, 1:2]).then_inc(k_ready, 1)
                    act.wait_ge(gb_ready, b + 1)
                    act.wait_ge(c_done, b + 1)
                    wait_ge(act, p_done, b)
                    act.activation(cT[:, :], ps_c[:, :], ACT.Tanh, bias=glo[:, 2:3]).then_inc(cT_ready, 1)
                    act.wait_ge(p_done, b + 1)
                    wait_ge(act, gate_ready, b)
                    act.activation(gates[:, :, :], ps_p[:, 0:NT * 2 * H].rearrange("p (t h) -> p t h", t=NT), ACT.Exp, scale=-1.0)\
                       .then_inc(exp_ready, 1)
                skewed(act, lambda b, u: front.scalar(act, b, u), back)

            @block.vector
            def _(dve):
                dve.tensor_tensor(bias_sum[:, :], sv.l1b_b[:, 2:3], sv.l1b_b[:, 3:4], ALU.add).then_inc(bias_ready, 1)
                dve.wait_ge(bias_ready, 1)

                def back(b, u):
                    dve.wait_ge(q_ready, b + 1)
                    dve.tensor_reduce(glo[:, 0:1], mixed[0][:, :], AX.X, ALU.add).then_inc(sum_ready, 1)
                    dve.wait_ge(sum_ready, b + 1)
                    wait_ge(dve, g_done, b)
                    dve.tensor_scalar(glo[:, 1:2], glo[:, 0:1], 1.0 / T, None, ALU.mult).then_inc(mean_ready, 1)
                    dve.tensor_scalar(scaled_q[:, :], mixed[0][:, :], -DH ** -0.5, None, ALU.mult).then_inc(scaled_ready, 1)
                    dve.wait_ge(g_done, b + 1)
                    wait_ge(dve, cT_ready, b)
                    dve.tensor_tensor(glo[:, 2:3], ps_g[:, 0:1], bias_sum[:, :], ALU.add).then_inc(gb_ready, 1)
                    dve.wait_ge(v_done, b + 1)
                    dve.tensor_tensor(sv.vtok[:, tiles_of(b), :], ps_v[:, :].rearrange("p (t d) -> p t d", t=NT),
                                      sv.bv[:, :].unsqueeze(1).to_broadcast([P, NT, D]), ALU.add).then_inc(v_ready, 1)
                    dve.wait_ge(scaled_ready, b + 1)
                    wait_ge(dve, stored[0], 16 * b)
                    split(dve, scaled_q[:, :], lambda i: parts[0][u][:, i, :], rest[0][:, :], split_steps[0], b)
                    dve.wait_ge(exp_ready, b + 1)
                    dve.tensor_scalar(gates[:, :, :], gates[:, :, :], 1.0, None, ALU.add).then_inc(one_ready, 1)
                    dve.wait_ge(one_ready, b + 1)
                    dve.reciprocal(gates[:, :, 0:H], gates[:, :, 0:H]).then_inc(recip_ready, 1)
                    dve.wait_ge(recip_ready, b + 1)
                    dve.scalar_tensor_tensor(out=sv.gates[:, tiles_of(b), 0:H], in0=gates[:, :, 0:H], scalar=-float(np.sqrt(2.0)),
                                             in1=gates[:, :, H:2 * H], op0=ALU.mult, op1=ALU.mult)
                    dve.tensor_scalar(sv.gates[:, tiles_of(b), H:2 * H], gates[:, :, H:2 * H], float(np.sqrt(2.0) / T), None, ALU.mult)\
                       .then_inc(gate_ready, 1)
                skewed(dve, lambda b, u: front.vector(dve, b, u), back)

            @block.gpsimd
            def _(pool):
                def back(b, u):
                    wait_alone(pool, sv, (k_ready, b + 1), (stored[1], 16 * b))
                    split(pool, mixed[1][:, :], lambda i: parts[1][u][:, i, :], rest[1][:, :], split_steps[1], b, alone=sv)
                skewed(pool, lambda b, u: front.pool(pool, b, u), back)

            @block.sync
            def _(sp):
                def store(b, u):
                    for i, to in enumerate((sv.q_parts, sv.k_parts)):
                        wait_alone(sp, sv, (split_steps[i], 4 * b + 4))
                        sp.wait_ge(stored[i], 16 * b)
                        sp.dma_start(to[bass.ds(b, 1), :, 0, :, :].rearrange("o i r t -> r (o i) t"), parts[i][u][:, :, :]).then_inc(stored[i], 16)
                with sp.Fori(0, NB // 2) as i:
                    store(2 * i, 0)
                    store(2 * i + 1, 1)
                for i in range(2):
                    sp.wait_ge(stored[i], 16 * NB)


def l1b_loads(sv):
    def loads(b, g, q_stack, k_stack):
        out = []
        for c, (kp, qp) in enumerate(COMBOS):
            for stack, parts, part in ((q_stack, sv.q_parts, qp), (k_stack, sv.k_parts, kp)):
                out.append((parts[bass.ds(b, 1), part, 0, g * GW:(g + 1) * GW, :].rearrange("o (h d) t -> (o d) h t", h=GH),
                            stack[c * DH:(c + 1) * DH, :, :]))
        return out
    return loads


def gated_attention_phase(nc, sv, tag, rows, loads):
    sv.tag = tag
    VW = 16
    TILES = GH * NT
    RING = 4
    N = NB * NG
    with nc.cleanup_on_exit():
        sb = nc.alloc_sbuf_tensor

        def sem(name):
            return nc.alloc_semaphore(f"{tag}_{name}")

        q_stack = [sb(f"{tag}_q_stack{u}", [rows, GH, T], BF16) for u in range(2)]
        k_stack = [sb(f"{tag}_k_stack{u}", [rows, GH, T], BF16) for u in range(2)]
        v_ones = [sb(f"{tag}_v_ones{u}", [P, NT, GH, VW], F32) for u in range(2)]
        gate = [sb(f"{tag}_gate{u}", [P, NT, 2, GH], F32) for u in range(2)]
        penalty = [sb(f"{tag}_penalty{r}", [P, T], F32) for r in range(RING)]
        minus_score = [sb(f"{tag}_minus_score{r}", [P, T], F32) for r in range(RING)]
        minus_max = [sb(f"{tag}_minus_max{u}", [P, TILES], F32) for u in range(2)]
        probs = [sb(f"{tag}_probs{r}", [P, T], F32) for r in range(RING)]
        probsT = [sb(f"{tag}_probsT{u}", [P, NT, GH, T], F32) for u in range(2)]
        ctxT = [sb(f"{tag}_ctxT{u}", [P, T], F32) for u in range(2)]
        inv = sb(f"{tag}_inv", [P, NT, GH], F32)
        ps_s = [nc.alloc_psum_tensor(f"{tag}_ps_s{r}", [P, 512], F32) for r in range(2)]
        ps_p = [nc.alloc_psum_tensor(f"{tag}_ps_p{r}", [P, 512], F32) for r in range(2)]
        ps_pv = [nc.alloc_psum_tensor(f"{tag}_ps_pv{u}", [P, 512], F32) for u in range(2)]
        ps_t = nc.alloc_psum_tensor(f"{tag}_ps_t", [P, 512], F32)
        prepared, zeroed, loaded = sem("prepared"), sem("zeroed"), [sem(f"loaded{u}") for u in range(2)]
        gate_copied, penalty_ready = sem("gate_copied"), sem("penalty_ready")
        s_done, score_ready, exp_done, p_turned = sem("s_done"), sem("score_ready"), sem("exp_done"), sem("p_turned")
        p_moved, pv_done, v_copied = sem("p_moved"), sem("pv_done"), sem("v_copied")
        ctxT_ready, turned, inv_ready, ctx_ready = sem("ctxT_ready"), sem("turned"), sem("inv_ready"), sem("ctx_ready")
        LOADS = len(loads(0, 0, q_stack[0], k_stack[0]))

        def before(n, k, lag):
            if k >= lag:
                return n, k - lag
            return None if isinstance(n, int) and n == 0 else (n - 1, k - lag + TILES)

        with nc.Block() as block:
            @block.sync
            def _(sp):
                def load(n, b, g):
                    wait_ge(sp, s_done, TILES * (n - 1))
                    for src, dst in loads(b, g, q_stack[g % 2], k_stack[g % 2]):
                        sp.dma_start(dst, src).then_inc(loaded[g % 2], 16)
                groups(sp, load)

            @block.gpsimd
            def _(pool):
                for u in range(2):
                    last = pool.memset(v_ones[u][:, :, :, :], 0.0)
                last.then_inc(prepared, 1)
                pool.wait_ge(prepared, 1)
                for u in range(2):
                    last = pool.memset(v_ones[u][:, :, :, DH:DH + 1], 1.0)
                last.then_inc(prepared, 1)
                pool.wait_ge(prepared, 2)

                def body(n, b, g):
                    wait_ge(pool, penalty_ready, TILES * (n - 1))
                    pool.tensor_copy(gate[g % 2][:, :, :, :],
                                     sv.gates[:, tiles_of(b), :].rearrange("p t (i h) -> p t i h", i=2)[:, :, :, g * GH:(g + 1) * GH])\
                        .then_inc(gate_copied, 1)
                    wait_ge(pool, pv_done, NT * (n - 1))
                    pool.tensor_copy(v_ones[g % 2][:, :, :, 0:DH],
                                     sv.vtok[:, tiles_of(b), g * GW:(g + 1) * GW].rearrange("p t (h d) -> p t h d", h=GH)).then_inc(v_copied, 1)
                groups(pool, body)

            @block.tensor
            def _(pe):
                pe.wait_ge(zeroed, 1)

                def turn_probs(n, k):
                    pe.wait_ge(exp_done, TILES * n + k + 1)
                    wait_ge(pe, p_moved, TILES * n + k - 1)
                    for c in range(NT):
                        last = pe.transpose(ps_p[k % 2][:, c * P:(c + 1) * P], probs[k % RING][:, c * P:(c + 1) * P], sv.ident[:, :])
                    last.then_inc(p_turned, 1)

                def pv(n, u, c):
                    if c == 0:
                        pe.wait_ge(p_moved, TILES * (n + 1))
                        pe.wait_ge(v_copied, n + 1)
                        wait_ge(pe, ctxT_ready, n - 1)
                    for h in range(GH):
                        last = pe.matmul(ps_pv[u][32 * h:32 * h + VW, :], v_ones[u][:, c, h, :], probsT[u][:, c, h, :],
                                         start=(c == 0), stop=(c == NT - 1))
                    last.then_inc(pv_done, 1)

                def turn_ctx(n, u):
                    pe.wait_ge(ctxT_ready, n + 1)
                    wait_ge(pe, ctx_ready, n)
                    for t in range(NT):
                        last = pe.transpose(ps_t[:, t * P:(t + 1) * P], ctxT[u][:, t * P:(t + 1) * P], sv.ident[:, :])
                    last.then_inc(turned, 1)

                def body(n, b, g):
                    u = g % 2
                    early = n if isinstance(n, int) else 2
                    pe.wait_ge(loaded[u], 16 * LOADS * (2 * b + g // 2 + 1))
                    for k in range(TILES):
                        h, t = divmod(k, NT)
                        wait_ge(pe, score_ready, TILES * n + k - 1)
                        pe.matmul(ps_s[k % 2][:, :], q_stack[u][:, h, t * P:(t + 1) * P], k_stack[u][:, h, :],
                                  start=True, stop=True).then_inc(s_done, 1)
                        if (at := before(n, k, 3)) is not None:
                            turn_probs(*at)
                        if early >= 1 and k in (5, 8, 11, 14):
                            pv(n - 1, 1 - u, (5, 8, 11, 14).index(k))
                        if early >= 2 and k == 3:
                            turn_ctx(n - 2, u)
                groups(pe, body)
                for k in range(TILES - 3, TILES):
                    turn_probs(N - 1, k)
                turn_ctx(N - 2, 0)
                for c in range(NT):
                    pv(N - 1, 1, c)
                turn_ctx(N - 1, 1)

            @block.scalar
            def _(act):
                def evacuate(n, u):
                    act.wait_ge(pv_done, NT * n + NT)
                    wait_ge(act, turned, n - 1)
                    act.activation(ctxT[u][:, :], ps_pv[u][:, :], ACT.Copy).then_inc(ctxT_ready, 1)

                def exponential(n, k, u):
                    act.wait_ge(score_ready, TILES * n + k + 1)
                    wait_ge(act, p_turned, TILES * n + k - RING + 1)
                    act.activation(probs[k % RING][:, :], minus_score[k % RING][:, :], ACT.Exp, bias=minus_max[u][:, k:k + 1], scale=-1.0)\
                       .then_inc(exp_done, 1)

                def body(n, b, g):
                    u = g % 2
                    for k in range(TILES):
                        h, t = divmod(k, NT)
                        if (at := before(n, k, 2)) is not None:
                            exponential(*at, u if k >= 2 else 1 - u)
                        if k == 0:
                            act.wait_ge(gate_copied, n + 1)
                        wait_ge(act, score_ready, TILES * n + k - RING + 1)
                        act.activation(penalty[k % RING][:, :], sv.positions[:, :], ACT.Square, bias=gate[u][:, t, 0, h:h + 1],
                                       scale=gate[u][:, t, 1, h:h + 1]).then_inc(penalty_ready, 1)
                        if k == 1 and not (isinstance(n, int) and n < 2):
                            evacuate(n - 2, u)
                groups(act, body)
                exponential(N - 1, TILES - 2, 1)
                exponential(N - 1, TILES - 1, 1)
                evacuate(N - 2, 0)
                evacuate(N - 1, 1)

            @block.vector
            def _(dve):
                for u in range(2):
                    last = dve.memset(ps_pv[u][:, :], 0.0)
                last.then_inc(zeroed, 1)

                def move(n, k, u):
                    h, t = divmod(k, NT)
                    dve.wait_ge(p_turned, TILES * n + k + 1)
                    wait_ge(dve, pv_done, NT * (n - 1))
                    dve.tensor_copy(probsT[u][:, :, h, t * P:(t + 1) * P], ps_p[k % 2][:, :].rearrange("p (c q) -> p c q", c=NT))\
                       .then_inc(p_moved, 1)

                def normalise(n, b, g):
                    dve.wait_ge(turned, n + 1)
                    raw = ps_t[:, :].rearrange("p (t h c) -> p t h c", t=NT, h=GH)
                    dve.reciprocal(inv[:, :, :], raw[:, :, :, DH]).then_inc(inv_ready, 1)
                    dve.wait_ge(inv_ready, n + 1)
                    dve.tensor_tensor(sv.ctx[:, tiles_of(b), g * GW:(g + 1) * GW].rearrange("p t (h d) -> p t h d", h=GH),
                                      raw[:, :, :, 0:DH], over(inv[:, :, :], P, NT, GH, DH), ALU.mult).then_inc(ctx_ready, 1)

                def body(n, b, g):
                    u = g % 2
                    for k in range(TILES):
                        wait_alone(dve, sv, (s_done, TILES * n + k + 1), (penalty_ready, TILES * n + k + 1),
                                   (exp_done, TILES * n + k - RING + 1))
                        dve.tensor_tensor_reduce(minus_score[k % RING][:, :], ps_s[k % 2][:, :], penalty[k % RING][:, :], 1.0, 3.0e38,
                                                 ALU.add, ALU.min, minus_max[u][:, k:k + 1]).then_inc(score_ready, 1)
                        if (at := before(n, k, 4)) is not None:
                            move(*at, u if k >= 4 else 1 - u)
                        if k == 6 and not (isinstance(n, int) and n < 2):
                            normalise(n - 2, b if g >= 2 else b - 1, (g - 2) % NG)
                groups(dve, body)
                for k in range(TILES - 4, TILES):
                    move(N - 1, k, 1)
                normalise(N - 2, NB - 1, NG - 2)
                normalise(N - 1, NB - 1, NG - 1)


class BankRing:

    def __init__(self, nc, tag, banks, names):
        self.banks = [nc.alloc_psum_tensor(f"{tag}_bank{i}", [P, 512], F32) for i in range(banks)]
        self.full = [nc.alloc_semaphore(f"{tag}_full{i}") for i in range(banks)]
        self.free = [nc.alloc_semaphore(f"{tag}_free{i}") for i in range(banks)]
        self.place = {n: (k % banks, k // banks) for k, n in enumerate(names)}
        self.held = [len(range(i, len(names), banks)) for i in range(banks)]

    def take(self, eng, name, b):
        i, k = self.place[name]
        wait_ge(eng, self.free[i], b * self.held[i] + k)
        return self.banks[i]

    def read(self, eng, name, b):
        i, k = self.place[name]
        eng.wait_ge(self.full[i], b * self.held[i] + k + 1)
        return self.banks[i]

    def moved(self, eng, name, b):
        i, k = self.place[name]
        eng.wait_ge(self.free[i], b * self.held[i] + k + 1)

    def is_full(self, instruction, name):
        instruction.then_inc(self.full[self.place[name][0]], 1)

    def is_free(self, instruction, name):
        instruction.then_inc(self.free[self.place[name][0]], 1)


def slot_attention_phase(nc, sv, tag):
    sv.tag = tag
    W2 = SH * SM
    HALF = SD // 2
    names = (["low"] + [f"proj{t}" for t in range(NT)] + [f"slot{t}" for t in range(NT)] + [f"z{t}" for t in range(NT)]
             + ["wvT0", "wvT1", "kT", "qT"] + [f"S{t}" for t in range(NT)] + ["L0", "L1", "pzT0", "pzT1"]
             + [f"A{t}" for t in range(NT)] + ["o", "ogT", "out"])
    with nc.cleanup_on_exit():
        def sb(name, shape, dt=F32):
            return nc.alloc_sbuf_tensor(f"{tag}_{name}", shape, dt)

        def sem(name):
            return nc.alloc_semaphore(f"{tag}_{name}")

        front = NormFront(nc, sv)
        ring = BankRing(nc, tag, 6, names)
        ps_state = nc.alloc_psum_tensor(f"{tag}_ps_state", [P, 512], F32)
        lowT = sb("lowT", [2 * LOW + 1, T])
        qkvg = sb("qkvg", [P, NT, 4 * D])
        clipped = sb("clipped", [P, NT, 2 * W2])
        w = sb("w", [P, NT, 2 * W2])
        w_sum = [None, None] + [sb(f"w_sum{t}", [P, 2 * W2]) for t in (2, 3)]
        rz = sb("rz", [P, NT, 2 * W2])
        products = [sb(f"rope_product{i}", [P, NT, 2 * SH, HALF]) for i in range(4)]
        qk = sb("qk", [P, NT, 2 * D])
        kT = sb("kT", [P, T])
        qD = sb("qD", [P, NT, SH, P])
        masked = sb("masked", [P, NT, SH, P])
        state = [None] + [sb(f"state{t}", [P, W2 + P]) for t in (1, 2, 3)]
        wvT = sb("wvT", [P, NT, 2, P])
        logits = sb("logits", [P, NT * SH, SM])
        top = sb("top", [P, NT * SH])
        expd = sb("expd", [P, NT * SH, SM])
        total = sb("total", [P, NT * SH])
        pz = sb("pz", [P, NT, W2])
        pD = sb("pD", [P, NT, SH, P])
        o = sb("o", [P, NT * SH, SD])
        o2 = sb("o2", [P, NT * SH, SD])
        ms = sb("ms", [P, 3, NT * SH])
        g_exp = sb("g_exp", [P, NT, D])
        g_gate = sb("g_gate", [P, NT, D])
        ogT = sb("ogT", [P, T])
        names_ = ("ones_set w_ready sum_ready rope_steps rope_ready state_done state_ready top_ready less_ready "
                  "exp_ready total_ready inv_ready pz_steps square_ready mean_ready rms_steps gexp_ready gone_ready "
                  "grecip_ready gate_steps on_ready og_ready").split()
        s = namedtuple("Signals", names_)(*[sem(n) for n in names_])
        last_bank, _ = ring.place[f"proj{NT - 1}"]
        front.xnT_used, front.uses = ring.free[last_bank], ring.held[last_bank]

        with nc.Block() as block:
            @block.tensor
            def _(pe):
                pe.wait_ge(s.ones_set, 1)

                def back(b, u):
                    xnT = front.xnT[u]
                    pe.wait_ge(front.xnT_ready, b + 1)
                    to = ring.take(pe, "low", b)
                    ring.is_full(pe.matmul(to[0:2 * LOW, :], sv.slot_w1[:, :], xnT[:, :], start=True, stop=True), "low")
                    for t in range(NT):
                        to = ring.take(pe, f"proj{t}", b)
                        ring.is_full(pe.matmul(to[:, :], xnT[:, t * P:(t + 1) * P], sv.slot_w[:, :], start=True, stop=True), f"proj{t}")
                    ring.moved(pe, "low", b)
                    for t in range(NT):
                        to = ring.take(pe, f"slot{t}", b)
                        ring.is_full(pe.matmul(to[:, :], lowT[:, t * P:(t + 1) * P], sv.slot_w2[:, :], start=True, stop=True), f"slot{t}")
                    for t in range(NT):
                        pe.wait_ge(s.w_ready, NT * b + t + 1)
                        to = ring.take(pe, f"z{t}", b)
                        last = pe.matmul(to[:, :], sv.causal[:, :], w[:, t, :], start=True, stop=(t == 0))
                        if t > 0:
                            if t > 1:
                                pe.wait_ge(s.sum_ready, 2 * b + t - 1)
                            last = pe.matmul(to[:, :], sv.ones[:, :], w[:, 0, :] if t == 1 else w_sum[t][:, :], start=False, stop=True)
                        ring.is_full(last, f"z{t}")
                    for i in range(2):
                        to = ring.take(pe, f"wvT{i}", b)
                        for j in range(4):
                            t, pair = 2 * i + j // 2, j % 2
                            last = pe.transpose(to[:, j * P:(j + 1) * P], w[:, t, W2 + pair * P:W2 + (pair + 1) * P], sv.ident[:, :])
                        ring.is_full(last, f"wvT{i}")
                    pe.wait_ge(s.rope_ready, b + 1)
                    for name, at in (("kT", D), ("qT", 0)):
                        to = ring.take(pe, name, b)
                        for t in range(NT):
                            last = pe.transpose(to[:, t * P:(t + 1) * P], qk[:, t, at:at + D], sv.ident[:, :])
                        ring.is_full(last, name)
                    ring.moved(pe, "kT", b)
                    for t in range(NT):
                        if t < NT - 1:
                            wait_ge(pe, s.state_ready, 3 * b + t)
                            pe.matmul(ps_state[:, 0:W2], qk[:, t, D:2 * D], w[:, t, 0:W2], start=(t == 0), stop=True, skip_group_check=True)
                            for pair in range(2):
                                last = pe.matmul(ps_state[:, W2 + pair * 64:W2 + (pair + 1) * 64], w[:, t, W2 + pair * P:W2 + (pair + 1) * P],
                                                 qkvg[:, t, 2 * D + pair * 64:2 * D + (pair + 1) * 64], start=False, stop=True,
                                                 skip_group_check=True)
                            last.then_inc(s.state_done, 1)
                        ring.moved(pe, "qT", b)
                        to = ring.take(pe, f"S{t}", b)
                        ring.is_full(pe.matmul(to[:, :], kT[:, t * P:(t + 1) * P], qD[:, t, :, :].rearrange("p h q -> p (h q)"),
                                               start=True, stop=True), f"S{t}")
                    pe.wait_ge(s.state_ready, 3 * b + 3)
                    for i in range(2):
                        to = ring.take(pe, f"L{i}", b)
                        for t in (2 * i, 2 * i + 1):
                            ring.moved(pe, f"S{t}", b)
                            for h in range(SH):
                                part = to[:, (t % 2) * W2 + h * SM:(t % 2) * W2 + (h + 1) * SM]
                                if t > 0:
                                    pe.matmul(part, qD[:, t, h, :], state[t][:, h * SM:(h + 1) * SM], start=True, stop=False)
                                last = pe.matmul(part, masked[:, t, h, :], w[:, t, h * SM:(h + 1) * SM], start=(t == 0), stop=True)
                        ring.is_full(last, f"L{i}")
                    pe.wait_ge(s.pz_steps, 2 * b + 2)
                    for i in range(2):
                        to = ring.take(pe, f"pzT{i}", b)
                        for j in range(4):
                            t, pair = 2 * i + j // 2, j % 2
                            last = pe.transpose(to[:, j * P:(j + 1) * P], pz[:, t, pair * P:(pair + 1) * P], sv.ident[:, :])
                        ring.is_full(last, f"pzT{i}")
                    ring.moved(pe, "wvT0", b)
                    ring.moved(pe, "wvT1", b)
                    for t in range(NT):
                        ring.moved(pe, f"pzT{t // 2}", b)
                        to = ring.take(pe, f"A{t}", b)
                        for pair in range(2):
                            last = pe.matmul(to[:, pair * 2 * P:(pair + 1) * 2 * P], wvT[:, t, pair, :],
                                             pD[:, t, 2 * pair:2 * pair + 2, :].rearrange("p h q -> p (h q)"), start=True, stop=True)
                        ring.is_full(last, f"A{t}")
                    to = ring.take(pe, "o", b)
                    for t in range(NT):
                        ring.moved(pe, f"A{t}", b)
                        for h in range(SH):
                            part = to[:, t * D + h * SD:t * D + (h + 1) * SD]
                            if t > 0:
                                pe.matmul(part, pD[:, t, h, :], state[t][:, W2 + h * SD:W2 + (h + 1) * SD], start=True, stop=False)
                            last = pe.matmul(part, masked[:, t, h, :], qkvg[:, t, 2 * D + h * SD:2 * D + (h + 1) * SD],
                                             start=(t == 0), stop=True)
                    ring.is_full(last, "o")
                    pe.wait_ge(s.og_ready, b + 1)
                    to = ring.take(pe, "ogT", b)
                    for t in range(NT):
                        last = pe.transpose(to[:, t * P:(t + 1) * P], o2[:, t * SH:(t + 1) * SH, :].rearrange("p h d -> p (h d)"), sv.ident[:, :])
                    ring.is_full(last, "ogT")
                    ring.moved(pe, "ogT", b)
                    to = ring.take(pe, "out", b)
                    for t in range(NT):
                        last = pe.matmul(to[:, t * D:(t + 1) * D], ogT[:, t * P:(t + 1) * P], sv.slot_wo[:, :], start=True, stop=True)
                    ring.is_full(last, "out")
                skewed(pe, lambda b, u: front.tensor(pe, b, u), back)

            @block.scalar
            def _(act):
                def back(b, u):
                    ps = ring.read(act, "low", b)
                    ring.is_free(act.activation(lowT[0:2 * LOW, :], ps[0:2 * LOW, :], ACT.Copy), "low")
                    for t in range(NT):
                        ps = ring.read(act, f"proj{t}", b)
                        ring.is_free(act.activation(qkvg[:, t, :], ps[:, :], ACT.Copy), f"proj{t}")
                    for t in range(NT):
                        ring.moved(act, f"slot{t}", b)
                        act.activation(w[:, t, :], clipped[:, t, :], ACT.Exp).then_inc(s.w_ready, 1)
                    for i in range(2):
                        ps = ring.read(act, f"wvT{i}", b)
                        ring.is_free(act.activation(wvT[:, 2 * i:2 * i + 2, :, :].rearrange("p t i q -> p (t i q)"), ps[:, :], ACT.Copy), f"wvT{i}")
                    ps = ring.read(act, "kT", b)
                    ring.is_free(act.activation(kT[:, :], ps[:, :], ACT.Copy), "kT")
                    for t in range(1, NT):
                        act.wait_ge(s.state_done, 3 * b + t)
                        act.activation(state[t][:, :], ps_state[:, 0:W2 + P], ACT.Copy).then_inc(s.state_ready, 1)
                    act.activation(g_exp[:, :, :], qkvg[:, :, 3 * D:4 * D], ACT.Exp, scale=-1.0).then_inc(s.gexp_ready, 1)
                    act.wait_ge(s.less_ready, b + 1)
                    act.activation(expd[:, :, :], logits[:, :, :], ACT.Exp, scale=float(SD ** -0.5)).then_inc(s.exp_ready, 1)
                    ps = ring.read(act, "o", b)
                    ring.is_free(act.activation(o[:, :, :], ps[:, :].rearrange("p (j d) -> p j d", d=SD), ACT.Copy), "o")
                    ps = ring.read(act, "ogT", b)
                    ring.is_free(act.activation(ogT[:, :], ps[:, :], ACT.Copy), "ogT")
                skewed(act, lambda b, u: front.scalar(act, b, u), back)

            @block.vector
            def _(dve):
                def back(b, u):
                    for t in range(NT):
                        ps = ring.read(dve, f"slot{t}", b)
                        ring.is_free(dve.tensor_scalar(clipped[:, t, :], ps[:, :], CLAMP, -CLAMP, ALU.min, ALU.max), f"slot{t}")
                    for t in range(NT):
                        ps = ring.read(dve, f"z{t}", b)
                        ring.is_free(dve.reciprocal(rz[:, t, :], ps[:, :]), f"z{t}")
                    ps = ring.read(dve, "qT", b)
                    for t in range(NT):
                        last = dve.tensor_tensor(qD[:, t, :, :], ps[:, t * P:(t + 1) * P].unsqueeze(1).to_broadcast([P, SH, P]),
                                                 over(sv.slot_mask[:, 0:SH], P, SH, P), ALU.mult)
                    ring.is_free(last, "qT")
                    causal = sv.causal[:, :].unsqueeze(1).to_broadcast([P, SH, P])
                    for t in range(NT):
                        ps = ring.read(dve, f"S{t}", b)
                        ring.is_free(dve.tensor_tensor(masked[:, t, :, :], ps[:, :].rearrange("p (h q) -> p h q", h=SH), causal, ALU.mult), f"S{t}")
                    for i in range(2):
                        ps = ring.read(dve, f"L{i}", b)
                        for t in (2 * i, 2 * i + 1):
                            ring.moved(dve, f"z{t}", b)
                        ring.is_free(dve.tensor_tensor(logits[:, i * 2 * SH:(i + 1) * 2 * SH, :].rearrange("p (t h) m -> p t (h m)", t=2),
                                                       ps[:, :].rearrange("p (t n) -> p t n", t=2), rz[:, 2 * i:2 * i + 2, 0:W2], ALU.mult), f"L{i}")
                    ring.moved(dve, "L0", b)
                    ring.moved(dve, "L1", b)
                    dve.tensor_reduce(top[:, :], logits[:, :, :], AX.X, ALU.max).then_inc(s.top_ready, 1)
                    dve.wait_ge(s.top_ready, b + 1)
                    dve.tensor_tensor(logits[:, :, :], logits[:, :, :], over(top[:, :], P, NT * SH, SM), ALU.subtract).then_inc(s.less_ready, 1)
                    dve.wait_ge(s.gexp_ready, b + 1)
                    dve.tensor_scalar(g_exp[:, :, :], g_exp[:, :, :], 1.0, None, ALU.add).then_inc(s.gone_ready, 1)
                    dve.wait_ge(s.gone_ready, b + 1)
                    dve.reciprocal(g_exp[:, :, :], g_exp[:, :, :]).then_inc(s.grecip_ready, 1)
                    dve.wait_ge(s.exp_ready, b + 1)
                    dve.tensor_reduce(total[:, :], expd[:, :, :], AX.X, ALU.add).then_inc(s.total_ready, 1)
                    dve.wait_ge(s.total_ready, b + 1)
                    dve.reciprocal(total[:, :], total[:, :]).then_inc(s.inv_ready, 1)
                    for i in range(2):
                        ps = ring.read(dve, f"pzT{i}", b)
                        for t in (2 * i, 2 * i + 1):
                            part = ps[:, (t % 2) * 2 * P:(t % 2 + 1) * 2 * P].rearrange("p (i q) -> p i q", i=2)
                            last = dve.tensor_tensor(pD[:, t, :, :].rearrange("p (i j) q -> p i j q", i=2),
                                                     part.unsqueeze(2).to_broadcast([P, 2, 2, P]),
                                                     sv.slot_mask[:, SH:SH + 2].unsqueeze(1).unsqueeze(3).to_broadcast([P, 2, 2, P]), ALU.mult)
                        ring.is_free(last, f"pzT{i}")
                    for t in range(NT):
                        ps = ring.read(dve, f"A{t}", b)
                        ring.is_free(dve.tensor_tensor(masked[:, t, :, :], ps[:, :].rearrange("p (h q) -> p h q", h=SH), causal, ALU.mult), f"A{t}")
                    dve.wait_ge(s.square_ready, b + 1)
                    dve.tensor_reduce(ms[:, 0, :], o2[:, :, :], AX.X, ALU.add).then_inc(s.mean_ready, 1)
                    dve.wait_ge(s.rms_steps, 2 * b + 2)
                    dve.tensor_tensor(o[:, :, :], o[:, :, :], over(ms[:, 2, :], P, NT * SH, SD), ALU.mult).then_inc(s.on_ready, 1)
                    dve.wait_ge(s.on_ready, b + 1)
                    dve.wait_ge(s.gate_steps, 2 * b + 2)
                    dve.tensor_tensor(o2[:, :, :], o[:, :, :], g_gate[:, :, :].rearrange("p t (h d) -> p (t h) d", d=SD), ALU.mult)\
                       .then_inc(s.og_ready, 1)
                    ps = ring.read(dve, "out", b)
                    x = sv.x[:, tiles_of(b), :]
                    ring.is_free(dve.tensor_tensor(x, ps[:, :].rearrange("p (t d) -> p t d", t=NT), x, ALU.add), "out")
                skewed(dve, lambda b, u: front.vector(dve, b, u), back)

            @block.gpsimd
            def _(pool):
                pool.memset(lowT[2 * LOW:2 * LOW + 1, :], 1.0).then_inc(s.ones_set, 1)
                pool.wait_ge(s.ones_set, 1)

                def back(b, u):
                    for t in range(NT):
                        ring.moved(pool, f"proj{t}", b)
                    halves = qkvg[:, :, 0:2 * D].rearrange("p t (j i c) -> p t j i c", i=2, c=HALF)
                    turned = qk[:, :, :].rearrange("p t (j i c) -> p t j i c", i=2, c=HALF)
                    cos, sin = [sv.rope[:, i, :].rearrange("p (t c) -> p t c", t=NT).unsqueeze(2).to_broadcast([P, NT, 2 * SH, HALF]) for i in range(2)]
                    for n, (i, table) in enumerate(((0, cos), (1, sin), (1, cos), (0, sin))):
                        pool.tensor_tensor(products[n][:, :, :, :], halves[:, :, :, i, :], table, ALU.mult).then_inc(s.rope_steps, 1)
                    pool.wait_ge(s.rope_steps, 4 * b + 4)
                    pool.tensor_tensor(turned[:, :, :, 0, :], products[0][:, :, :, :], products[1][:, :, :, :], ALU.subtract)
                    pool.tensor_tensor(turned[:, :, :, 1, :], products[2][:, :, :, :], products[3][:, :, :, :], ALU.add).then_inc(s.rope_ready, 1)
                    pool.wait_ge(s.w_ready, NT * b + 3)
                    pool.tensor_tensor(w_sum[2][:, :], w[:, 0, :], w[:, 1, :], ALU.add).then_inc(s.sum_ready, 1)
                    pool.wait_ge(s.sum_ready, 2 * b + 1)
                    pool.tensor_tensor(w_sum[3][:, :], w_sum[2][:, :], w[:, 2, :], ALU.add).then_inc(s.sum_ready, 1)
                    pool.wait_ge(s.grecip_ready, b + 1)
                    pool.tensor_tensor(g_gate[:, :, :], g_exp[:, :, :], qkvg[:, :, 3 * D:4 * D], ALU.mult).then_inc(s.gate_steps, 1)
                    pool.wait_ge(s.gate_steps, 2 * b + 1)
                    pool.tensor_tensor(g_gate[:, :, :].rearrange("p t (h d) -> p (t h) d", d=SD), g_gate[:, :, :].rearrange("p t (h d) -> p (t h) d", d=SD),
                                       sv.gnorm[:, :].unsqueeze(1).to_broadcast([P, NT * SH, SD]), ALU.mult).then_inc(s.gate_steps, 1)
                    pool.wait_ge(s.inv_ready, b + 1)
                    pool.tensor_tensor(expd[:, :, :], expd[:, :, :], over(total[:, :], P, NT * SH, SM), ALU.mult).then_inc(s.pz_steps, 1)
                    pool.wait_ge(s.pz_steps, 2 * b + 1)
                    for t in range(NT):
                        ring.moved(pool, f"z{t}", b)
                    pool.tensor_tensor(pz[:, :, :], expd[:, :, :].rearrange("p (t h) m -> p t (h m)", t=NT), rz[:, :, W2:2 * W2], ALU.mult)\
                        .then_inc(s.pz_steps, 1)
                    ring.moved(pool, "o", b)
                    pool.tensor_tensor(o2[:, :, :], o[:, :, :], o[:, :, :], ALU.mult).then_inc(s.square_ready, 1)
                    wait_alone(pool, sv, (s.mean_ready, b + 1))
                    pool.tensor_scalar(ms[:, 1, :], ms[:, 0, :], 1.0 / SD, EPS, ALU.mult, ALU.add).then_inc(s.rms_steps, 1)
                    pool.wait_ge(s.rms_steps, 2 * b + 1)
                    pool.tensor_tensor(ms[:, 2, :], ms[:, 1, :], sv.minus_half[:, 0:NT * SH], ALU.pow).then_inc(s.rms_steps, 1)
                skewed(pool, lambda b, u: front.pool(pool, b, u), back)


_INS = []


def constants():
    f = np.float32
    rows = np.arange(P)
    pos = np.arange(T, dtype=f)
    block = (rows[:, None] // DH == rows[None, :] // DH).astype(f) * f(DH ** -0.5)
    ind = (rows[:, None] // DH == np.arange(H)[None, :]).astype(f)
    causal = (rows[:, None] <= rows[None, :]).astype(f)
    slot_mask = np.concatenate([rows[:, None] // SD == np.arange(SH)[None, :], rows[:, None] // SM == np.arange(2)[None, :]], 1).astype(f)
    half = SD // 2
    inv = (f(1.0) / f(10000.0) ** (np.arange(half, dtype=f) / f(half))).astype(f)
    ang = (pos[:, None] * inv[None, :]).astype(f)
    rope = np.stack([np.cos(ang), np.sin(ang)], 0).astype(f)
    rope = rope.reshape(2, NT, P, half).transpose(2, 0, 1, 3).reshape(P, 2, NT * half)
    freqs = (f(10000.0) ** (-(np.arange(DH, dtype=f) / f(DH)))).astype(f)
    ang = (freqs[rows % DH][:, None] * pos[None, :]).astype(f)
    pope = np.stack([np.cos(ang), np.sin(ang)], 1).astype(f)
    return {
        "c_ident": np.eye(P, dtype=f), "c_block_mask": block, "c_head_ind": ind, "c_causal": causal, "c_slot_mask": slot_mask,
        "c_positions": np.broadcast_to(pos, (P, T)).copy(), "c_rope": np.ascontiguousarray(rope), "c_pope": np.ascontiguousarray(pope),
    }


def program(nc, a, out):
    sv = Shared()
    sb = nc.alloc_sbuf_tensor
    sv.x = sb("x", [P, NB * NT, D], F32)
    sv.ctx = sb("ctx", [P, NB * NT, D], F32)
    sv.vtok = sb("vtok", [P, NB * NT, D], F32)
    sv.ident = sb("ident", [P, P], F32)
    sv.block_mask = sb("block_mask", [P, P], F32)
    sv.head_ind = sb("head_ind", [P, H], F32)
    sv.causal = sb("causal", [P, P], F32)
    sv.positions = sb("positions", [P, T], F32)
    sv.rope = sb("rope", [P, 2, NT * SD // 2], F32)
    sv.pope_table = sb("pope_table", [P, 2, T], F32)
    sv.pope_bias = sb("pope_bias", [P, 1], F32)
    sv.minus_half = sb("minus_half", [P, 64], F32)
    sv.ones = sb("ones", [P, P], F32)
    sv.ident_bf = sb("ident_bf", [P, P], BF16)
    sv.ffn0_w = sb("ffn0_w", [P, D + E * R + E], F32)
    sv.lora_b = sb("lora_b", [P, D], F32)
    sv.router_bias = sb("router_bias", [P, E], F32)
    sv.base_bias = sb("base_bias", [P, D], F32)
    sv.bv = sb("bv", [P, D], F32)
    sv.bo = sb("bo", [P, D], F32)
    sv.gnorm = sb("gnorm", [P, SD], F32)
    sv.gate = sb("gate", [P, 1], F32)
    sv.l0b_w = sb("l0b_w", [P, 4, D], F32)
    sv.l1a_wk = sb("l1a_wk", [P, D], F32)
    sv.l1a_wo = sb("l1a_wo", [P, D], F32)
    sv.ffn1_fc = sb("ffn1_fc", [P, HID], F32)
    sv.ffn1_proj = sb("ffn1_proj", [P, NK, D], F32)
    sv.slot_w = sb("slot_w", [P, 4 * D], F32)
    sv.slot_wo = sb("slot_wo", [P, D], F32)
    sv.slot_mask = sb("slot_mask", [P, SH + 2], F32)
    sv.slot_w1 = sb("slot_w1", [P, 2 * LOW], F32)
    sv.slot_w2 = sb("slot_w2", [2 * LOW + 1, 2 * SH * SM], F32)
    sv.l1b_w = sb("l1b_w", [P, 6, D], F32)
    sv.l1b_b = sb("l1b_b", [P, 4], F32)
    sv.l1b_u = sb("l1b_u", [P, 2], F32)
    sv.gates = sb("gates", [P, NB * NT, 2 * H], F32)
    sv.l1b_up = sb("l1b_up", [P, 2 * H], F32)
    sv.past = nc.alloc_semaphore("past")
    sv.q_parts = nc.dram_tensor("q_parts", (NB, 3, 2, P, T), BF16).ap()
    sv.k_parts = nc.dram_tensor("k_parts", (NB, 3, 2, P, T), BF16).ap()
    sv.n_parts = nc.dram_tensor("n_parts", (NB, 3, H, T), BF16).ap()
    load_phase(nc, sv, a)
    slot_attention_phase(nc, sv, "s1")
    ffn0_phase(nc, sv, "f2")
    l0b_prep_phase(nc, sv, "p3")
    attention_phase(nc, sv, "a3", 12 * DH, l0b_loads(sv), with_max=True)
    ffn0_phase(nc, sv, "f4", wo=sv.l0b_w[:, 3, :])
    l1a_prep_phase(nc, sv, "p5")
    attention_phase(nc, sv, "a5", 6 * DH + 6, l1a_loads(sv), ones_from=32)
    ffn1_phase(nc, sv, "f6", wo=sv.l1a_wo[:, :])
    l1b_prep_phase(nc, sv, "p7")
    gated_attention_phase(nc, sv, "a7", 6 * DH, l1b_loads(sv))
    ffn1_phase(nc, sv, "f8", wo=sv.l1b_w[:, 3, :], bo=sv.bo[:, :], out=out)


def kernel(**inputs):
    import concourse.bacc as bacc
    from concourse.bass_utils import run_bass_kernel_spmd

    nc = bacc.Bacc("TRN2", target_bir_lowering=False, num_devices=1)
    arrays, args = {}, {}
    shaped = {name: np.ascontiguousarray(v) for name, v in inputs.items()}
    shaped["L1_ffn_gate"] = shaped["L1_ffn_gate"].reshape(1)
    shaped.update(constants())
    for name, v in shaped.items():
        arrays[f"in_{name}"] = v
        args[name] = nc.dram_tensor(f"in_{name}", v.shape, mybir.dt.from_np(v.dtype), kind="ExternalInput").ap()
    out = nc.dram_tensor("out", (NB, T, D), F32, kind="ExternalOutput").ap()
    program(nc, args, out)
    return run_bass_kernel_spmd(nc, [arrays], core_ids=[0]).results[0]["out"]
```
